# Optimizing a Trainium2 kernel written in Bass

```python
import numpy as np
import jax
import jax.numpy as jnp

def _softmax(x, axis=-1):
    return jax.nn.softmax(x, axis=axis)

def _gelu(x):
    return jax.nn.gelu(x, approximate=True)

def _silu(x):
    return jax.nn.silu(x)

def _sigmoid(x):
    return jax.nn.sigmoid(x)

def _layernorm(x, axis=-1, eps=1e-05):
    m = jnp.mean(x, axis=axis, keepdims=True)
    v = jnp.var(x, axis=axis, keepdims=True)
    return (x - m) / jnp.sqrt(v + eps)

def _scatter_add(tgt, idx, src, axis=0):
    return tgt.at[idx].add(src)

def _segment_sum(src, seg, n):
    return jax.ops.segment_sum(src, seg, n)
kernel_name = 'mk_prb_d1_jaxref_r8_bd2c1e'

def setup_inputs(seed: int=0):
    np.random.seed(seed)
    _w = jnp.asarray

    def _L0_attn_setup():
        import jax, jax.numpy as jnp
        import numpy as np
        D_MODEL = 128
        N_HEADS = 16
        D_HEAD = 64
        VAR_EPS = 1e-05
        INIT_RANGE = 0.02
        B, S = (2, 256)

        def _layernorm(x, w, b):
            mean = jnp.mean(x, axis=-1, keepdims=True)
            var = jnp.var(x, axis=-1, keepdims=True)
            norm = (x - mean) / jnp.sqrt(var + VAR_EPS)
            return norm * w + b
        key = jax.random.key(seed)
        ks = jax.random.split(key, 6)
        resid_stream = jax.random.normal(ks[0], (B, S, D_MODEL), dtype=jnp.float32)
        attn_mask = jnp.ones((B, S), dtype=jnp.int32)
        W_q = jax.random.normal(ks[1], (N_HEADS, D_MODEL, D_HEAD), dtype=jnp.float32) * INIT_RANGE
        W_k = jax.random.normal(ks[2], (N_HEADS, D_MODEL, D_HEAD), dtype=jnp.float32) * INIT_RANGE
        W_v = jax.random.normal(ks[3], (N_HEADS, D_MODEL, D_HEAD), dtype=jnp.float32) * INIT_RANGE
        W_o = jax.random.normal(ks[4], (N_HEADS, D_HEAD, D_MODEL), dtype=jnp.float32) * INIT_RANGE
        b_q = jnp.zeros((N_HEADS, D_HEAD), dtype=jnp.float32)
        b_k = jnp.zeros((N_HEADS, D_HEAD), dtype=jnp.float32)
        b_v = jnp.zeros((N_HEADS, D_HEAD), dtype=jnp.float32)
        b_o = jnp.zeros((D_MODEL,), dtype=jnp.float32)
        ln_w = jnp.ones((D_MODEL,), dtype=jnp.float32)
        ln_b = jnp.zeros((D_MODEL,), dtype=jnp.float32)
        return dict(resid_stream=resid_stream, attn_mask=attn_mask, W_q=W_q, W_k=W_k, W_v=W_v, W_o=W_o, b_q=b_q, b_k=b_k, b_v=b_v, b_o=b_o, ln_w=ln_w, ln_b=ln_b)
    _L0_attn_in = _L0_attn_setup()

    def _L0_ffn_setup():
        import jax, jax.numpy as jnp
        import numpy as np
        EPS = 1e-05

        def _quantize(W):
            gamma = jnp.mean(jnp.abs(W))
            return jnp.clip(jnp.round(W / (gamma + EPS)), -1.0, 1.0)
        key = jax.random.key(seed)
        k_x, k_w1, k_b1, k_w2, k_b2 = jax.random.split(key, 5)
        n_embd = 128
        d_ff = 4 * n_embd
        B, S = (4, 512)
        bound1 = 1.0 / np.sqrt(n_embd)
        bound2 = 1.0 / np.sqrt(d_ff)
        x = jax.random.normal(k_x, (B, S, n_embd), dtype=jnp.float32)
        W1 = jax.random.uniform(k_w1, (d_ff, n_embd), jnp.float32, -bound1, bound1)
        b1 = jax.random.uniform(k_b1, (d_ff,), jnp.float32, -bound1, bound1)
        W2 = jax.random.uniform(k_w2, (n_embd, d_ff), jnp.float32, -bound2, bound2)
        b2 = jax.random.uniform(k_b2, (n_embd,), jnp.float32, -bound2, bound2)
        return {'x': x, 'W1': W1, 'b1': b1, 'W2': W2, 'b2': b2}
    _L0_ffn_in = _L0_ffn_setup()
    _d = {'L0_attn_resid_stream': _L0_attn_in['resid_stream'], 'L0_attn_attn_mask': _L0_attn_in['attn_mask'], 'L0_attn_W_q': _L0_attn_in['W_q'], 'L0_attn_W_k': _L0_attn_in['W_k'], 'L0_attn_W_v': _L0_attn_in['W_v'], 'L0_attn_W_o': _L0_attn_in['W_o'], 'L0_attn_b_q': _L0_attn_in['b_q'], 'L0_attn_b_k': _L0_attn_in['b_k'], 'L0_attn_b_v': _L0_attn_in['b_v'], 'L0_attn_b_o': _L0_attn_in['b_o'], 'L0_attn_ln_w': _L0_attn_in['ln_w'], 'L0_attn_ln_b': _L0_attn_in['ln_b'], 'L0_ffn_W1': _L0_ffn_in['W1'], 'L0_ffn_b1': _L0_ffn_in['b1'], 'L0_ffn_W2': _L0_ffn_in['W2'], 'L0_ffn_b2': _L0_ffn_in['b2']}
    _x0 = _d['L0_attn_resid_stream']
    _d['L0_attn_resid_stream'] = jax.random.normal(jax.random.fold_in(jax.random.key(seed), 1), (8, 256, 128), dtype=_x0.dtype)
    del _x0
    return _d

def reference(L0_attn_resid_stream, L0_attn_attn_mask, L0_attn_W_q, L0_attn_W_k, L0_attn_W_v, L0_attn_W_o, L0_attn_b_q, L0_attn_b_k, L0_attn_b_v, L0_attn_b_o, L0_attn_ln_w, L0_attn_ln_b, L0_ffn_W1, L0_ffn_b1, L0_ffn_W2, L0_ffn_b2):

    def _L0_attn_ref(resid_stream, attn_mask, W_q, W_k, W_v, W_o, b_q, b_k, b_v, b_o, ln_w, ln_b):
        import jax, jax.numpy as jnp
        import numpy as np
        D_MODEL = 128
        N_HEADS = 16
        D_HEAD = 64
        VAR_EPS = 1e-05
        INIT_RANGE = 0.02
        B, S = (2, 256)

        def _layernorm(x, w, b):
            mean = jnp.mean(x, axis=-1, keepdims=True)
            var = jnp.var(x, axis=-1, keepdims=True)
            norm = (x - mean) / jnp.sqrt(var + VAR_EPS)
            return norm * w + b
        x = _layernorm(resid_stream, ln_w, ln_b)
        q = jnp.einsum('bsd,hde->bshe', x, W_q) + b_q
        k = jnp.einsum('bsd,hde->bshe', x, W_k) + b_k
        v = jnp.einsum('bsd,hde->bshe', x, W_v) + b_v
        scale = D_HEAD ** (-0.5)
        scores = jnp.einsum('bqhe,bkhe->bhqk', q, k) * scale
        sq, sk = (scores.shape[-2], scores.shape[-1])
        causal = jnp.tril(jnp.ones((sq, sk), dtype=bool))
        scores = jnp.where(causal, scores, -jnp.inf)
        pattern = jax.nn.softmax(scores, axis=-1)
        z = jnp.einsum('bhqk,bkhe->bqhe', pattern, v)
        attn_out = jnp.einsum('bqhe,hed->bqd', z, W_o) + b_o
        return attn_out

    def _L0_ffn_ref(x, W1, b1, W2, b2):
        import jax, jax.numpy as jnp
        import numpy as np
        EPS = 1e-05

        def _quantize(W):
            gamma = jnp.mean(jnp.abs(W))
            return jnp.clip(jnp.round(W / (gamma + EPS)), -1.0, 1.0)
        Wq1 = _quantize(W1)
        Wq2 = _quantize(W2)
        h = jax.nn.relu(jnp.einsum('bsd,fd->bsf', x, Wq1) + b1)
        out = jnp.einsum('bsf,df->bsd', h, Wq2) + b2
        return out
    x = L0_attn_resid_stream
    xn = _layernorm(x, axis=-1)
    x = x + _L0_attn_ref(xn, L0_attn_attn_mask, L0_attn_W_q, L0_attn_W_k, L0_attn_W_v, L0_attn_W_o, L0_attn_b_q, L0_attn_b_k, L0_attn_b_v, L0_attn_b_o, L0_attn_ln_w, L0_attn_ln_b) + _L0_ffn_ref(xn, L0_ffn_W1, L0_ffn_b1, L0_ffn_W2, L0_ffn_b2)
    return x

_drawn_inputs = setup_inputs


def setup_inputs(seed=0):
    import zlib

    import numpy as np

    out = dict(_drawn_inputs(seed))
    spreads = {'L0_attn_b_q': (0.0, 0.8),
     'L0_attn_b_k': (0.0, 2.0),
     'L0_attn_b_v': (0.0, 2.0),
     'L0_attn_b_o': (0.0, 2.0),
     'L0_attn_ln_w': (1.0, 0.6),
     'L0_attn_ln_b': (0.0, 0.8)}
    factors = {'L0_attn_W_q': 8.0,
     'L0_attn_W_k': 8.0,
     'L0_attn_W_v': 8.0,
     'L0_attn_W_o': 8.0,
     'L0_ffn_b1': 8.0,
     'L0_ffn_b2': 200.0}
    for name, (base, spread) in spreads.items():
        noise = np.random.default_rng([zlib.crc32(name.encode()), seed]).standard_normal(out[name].shape)
        drawn = base * np.exp(spread * noise) if base else spread * noise
        out[name] = jnp.asarray(drawn.astype(out[name].dtype))
    for name, factor in factors.items():
        out[name] = (out[name] * factor).astype(out[name].dtype)
    return out
```

```python
import numpy as np
import concourse.bass as bass
from concourse import mybir
from contextlib import ExitStack


F32 = mybir.dt.float32
F32R = mybir.dt.float32r
ACT = mybir.ActivationFunctionType
ALU = mybir.AluOpType
AX = mybir.AxisListType

P = 128
B, S, D = 8, 256, 128
H, E = 16, 64
FF = 512
EPS = 1e-5
PAIRS = H // 2
TILES = S // P
NT = B * TILES
FC = FF // P
SCALE = E ** -0.5
MASKED = -3.0e38
LAG = 2
NP_BUF = 4
NPT_BUF = 2
REGULAR = 2

UNITS = [
    [("q", 2, 0), ("k", 2, 0), ("v", (0, 1), 0), ("z", 6, -1)],
    [("q", 3, 0), ("k", 3, 0), ("z", 7, -1)],
    [("q", 4, 0), ("k", 4, 0), ("o", 0, -1), ("o", 1, -1), ("z", 0, 0)],
    [("q", 5, 0), ("k", 5, 0), ("v", (1, 0), 0), ("f", 0, 0), ("z", 1, 0)],
    [("q", 6, 0), ("k", 6, 0), ("v", (1, 1), 0), ("f", 1, 0), ("z", 2, 0)],
    [("q", 7, 0), ("k", 7, 0), ("f", 2, 0), ("f", 3, 0), ("x", "n", 1), ("x", "h", 1), ("z", 3, 0)],
    [("q", 0, 1), ("k", 0, 1), ("z", 4, 0)],
    [("q", 1, 1), ("k", 1, 1), ("v", (0, 0), 1), ("z", 5, 0)],
]
COPIER = {"q": "act", "k": "act", "v": "dve", "f": "act", "x": "dve", "o": "dve", "z": "dve"}
PER_BATCH = sum(len(u) for u in UNITS)


def all_units():
    out = []
    for b in range(-1, B + 1):
        n = 0
        for i in range(PAIRS):
            for kind, index, off in UNITS[i]:
                if 0 <= b + off < B:
                    out.append((b, i, kind, index, b + off, n % 2))
                n += 1
    return out


ALL = all_units()
WHERE = {(u[2], u[3], u[4]): n for n, u in enumerate(ALL)}


def units_done(n):
    return n + 1


def copies_done(n):
    who = COPIER[ALL[n][2]]
    return who, sum(COPIER[u[2]] == who for u in ALL[:n + 1])


def same_bank_before(n):
    return next((m for m in range(n - 1, -1, -1) if ALL[m][5] == ALL[n][5]), None)


COPIES_PER_BATCH = {w: sum(COPIER[k] == w for u in UNITS for k, _, _ in u) for w in ("act", "dve")}


def attention_ffn_kernel(nc, resid, attn_mask, w_q, w_k, w_v, w_o, b_q, b_k, b_v, b_o, ln_w, ln_b,
                         w1, b1, w2, b2, out):
    ctx = ExitStack()
    with ctx:
        def sb(name, shape, dt=F32):
            return ctx.enter_context(nc.sbuf_tensor(name, shape, dt))

        def sem(name):
            return ctx.enter_context(nc.semaphore(name))

        ident = sb("ident", [P, P])
        ones = sb("ones", [P, P])
        tri = sb("tri", [P, 2, P])
        wq_raw = sb("wq_raw", [P, H * E])
        wk_raw = sb("wk_raw", [P, H * E])
        wv_raw = sb("wv_raw", [P, H * E])
        raw = {"q": wq_raw, "k": wk_raw, "v": wv_raw}
        whi = {n: sb(f"w{n}_hi", [P, H * E], F32R) for n in "qkv"}
        wlo = {n: sb(f"w{n}_lo", [P, H * E], F32R) for n in "qkv"}
        wo = sb("wo", [P, PAIRS, D])
        w1_raw = sb("w1_raw", [P, FC, D])
        w2_raw = sb("w2_raw", [D, FF])
        w_abs = sb("w_abs", [P, FF])
        w_below = sb("w_below", [P, FF])
        w1_tern = sb("w1_tern", [P, FC, D])
        w2_tern = sb("w2_tern", [D, FF])
        w1T = sb("w1T", [D, FC, P], F32R)
        w2T = sb("w2T", [P, FC, D])
        abs_sum = sb("abs_sum", [P, 2])
        thr = sb("thr", [P, 2])
        nthr = sb("nthr", [P, 2])
        NVEC = 2 * PAIRS + 2 + FC
        vec_rows = sb("vec_rows", [NVEC, P])
        vecs = sb("vecs", [P, NVEC])
        BQ, BK, LW, LB, B1 = 0, PAIRS, 2 * PAIRS, 2 * PAIRS + 1, 2 * PAIRS + 2
        bv_all = sb("bv_all", [P, H * E])
        bo_all = sb("bo_all", [P, D])
        b2_all = sb("b2_all", [P, D])
        bias_out = sb("bias_out", [P, D])

        x_all = sb("x_all", [P, NT, D])
        x_res = sb("x_res", [P, NT, D])
        xn_all = sb("xn_all", [P, NT, D])
        stats = sb("stats", [P, NT, 6])
        mv1 = sb("mv1", [P, NT, 2])
        mv2 = sb("mv2", [P, NT, 2])
        veps = sb("veps", [P, NT])
        std = sb("std", [P, NT])
        r1 = sb("r1", [P, NT])
        r2 = sb("r2", [P, NT])
        xn_cur = sb("xn_cur", [P, TILES, D])
        xh_cur = sb("xh_cur", [P, TILES, D])
        xnT_hi = sb("xnT_hi", [D, S], F32R)
        xnT_lo = sb("xnT_lo", [D, S], F32R)
        x2T = sb("x2T", [D, S])
        x2T_hi = sb("x2T_hi", [D, S], F32R)
        x2T_lo = sb("x2T_lo", [D, S], F32R)
        qT = sb("qT", [P, PAIRS, S])
        kT = sb("kT", [P, PAIRS, S])
        v = sb("v", [P, TILES, H * E])
        hT = sb("hT", [P, FC, S])
        zT = sb("zT", [P, PAIRS, S])
        out_sb = sb("out_sb", [P, TILES, D])

        W = S + P
        prob = sb("prob", [P, NP_BUF, 2, W])
        pT_wide = sb("pT_wide", [P, NPT_BUF, 2, S])
        pT_narrow = sb("pT_narrow", [P, NPT_BUF, 2, P])
        row_max = sb("row_max", [P, NP_BUF, 4])
        neg_max = sb("neg_max", [P, NP_BUF, 4])
        row_sum = sb("row_sum", [P, NP_BUF, 4])
        inv_sum = sb("inv_sum", [P, NP_BUF, 4])

        s_ps = ctx.enter_context(nc.psum_tensor("s_ps", [P, 2, 2, 512], F32))
        ptw_ps = ctx.enter_context(nc.psum_tensor("ptw_ps", [P, 2, S], F32))
        ptn_ps = ctx.enter_context(nc.psum_tensor("ptn_ps", [P, 512], F32))
        m_ps = [ctx.enter_context(nc.psum_tensor(f"m_ps{n}", [P, 512], F32)) for n in range(2)]

        x_in = [sem("x_in0"), sem("x_in1")]
        w_in = {n: sem(f"w{n}_in") for n in "qkv"}
        wo_in = sem("wo_in")
        w12_in = sem("w12_in")
        vec_in = sem("vec_in")
        bias_in = sem("bias_in")
        consts = sem("consts")
        pool_chain = sem("pool_chain")
        dve_chain = sem("dve_chain")
        act_chain = sem("act_chain")
        w_hi_done = sem("w_hi_done")
        w_lo_done = sem("w_lo_done")
        var_ready = sem("var_ready")
        std_ready = sem("std_ready")
        vecs_T = sem("vecs_T")
        vecs_ready = sem("vecs_ready")
        abs_ready = sem("abs_ready")
        abs_total = sem("abs_total")
        tern_ready = sem("tern_ready")
        w1T_ready = sem("w1T_ready")
        w2T_ready = sem("w2T_ready")
        ffn_w_ready = sem("ffn_w_ready")
        res_ready = sem("res_ready")
        norm_ready = sem("norm_ready")
        scores_ready = sem("scores_ready")
        max_ready = sem("max_ready")
        exp_done = sem("exp_done")
        inv_ready = sem("inv_ready")
        prob_ready = sem("prob_ready")
        ptw_ready = sem("ptw_ready")
        ptn_ready = sem("ptn_ready")
        ptw_copied = sem("ptw_copied")
        ptn_copied = sem("ptn_copied")
        units_ready = sem("units_ready")
        act_copied = sem("act_copied")
        dve_copied = sem("dve_copied")
        copied = {"act": act_copied, "dve": dve_copied}
        xnhi_ready = sem("xnhi_ready")
        x2_ready = sem("x2_ready")
        x2hi_ready = sem("x2hi_ready")
        masked = sem("masked")
        maxed = sem("maxed")
        out_done = sem("out_done")

        def at(b, rep, value, per_batch):
            return value if isinstance(b, int) else b * per_batch + (value - rep * per_batch)

        def wait(eng, s, b, rep, value, per_batch):
            if value > 0:
                eng.wait_ge(s, at(b, rep, value, per_batch))

        def wait_slot(eng, s, b, rep, slot):
            wait(eng, s, b, rep, PAIRS * rep + slot + 1, PAIRS)

        def wait_unit(eng, b, rep, n):
            wait(eng, units_ready, b, rep, units_done(n), PER_BATCH)

        def wait_copy(eng, b, rep, n):
            who, value = copies_done(n)
            wait(eng, copied[who], b, rep, value, COPIES_PER_BATCH[who])

        def slot_units(rep, i):
            return [(n, u) for n, u in enumerate(ALL) if u[0] == rep and u[1] == i]

        def batches(eng, body):
            for b in range(-1, REGULAR):
                body(b, b)
            with eng.Fori(REGULAR, B - 1) as b:
                body(b, REGULAR)
            body(B - 1, B - 1)
            body(B, B)

        def has_scores(rep):
            return 0 <= rep < B

        def has_tail(rep, i):
            return 0 <= PAIRS * rep + i - LAG < PAIRS * B

        block = ctx.enter_context(nc.Block())

        @block.sync
        def _(sp):
            x_v = resid.rearrange("b (t p) d -> p (b t) d", p=P)
            sp.dma_start(x_all[:, 0:TILES, :], x_v[:, 0:TILES, :]).then_inc(x_in[0], 16)
            for n, w in (("q", w_q), ("k", w_k)):
                sp.dma_start(raw[n][:, :].rearrange("d (h e) -> d h e", h=H),
                             w.rearrange("h d e -> d h e")).then_inc(w_in[n], 16)
            sp.dma_start(x_all[:, TILES:NT, :], x_v[:, TILES:NT, :]).then_inc(x_in[1], 16)
            sp.dma_start(bo_all[:, :], b_o.rearrange("(a d) -> a d", a=1).broadcast_to([P, D])).then_inc(bias_in, 16)
            sp.dma_start(b2_all[:, :], b2.rearrange("(a d) -> a d", a=1).broadcast_to([P, D])).then_inc(bias_in, 16)
            out_v = out.rearrange("b (t p) d -> b p t d", p=P)

            def body(b, rep):
                if not 1 <= rep:
                    return
                wait_copy(sp, b, rep, WHERE["o", 1, rep - 1])
                sp.dma_start(out_v[b - 1], out_sb[:, :, :]).then_inc(out_done, 16)
            batches(sp, body)
            sp.wait_ge(out_done, 16 * B)

        @block.gpsimd
        def _(pool):
            nc.gpsimd.memset(ident[:, :], 0.0).then_inc(pool_chain, 1)
            nc.gpsimd.memset(tri[:, :, :], 0.0).then_inc(pool_chain, 1)
            nc.gpsimd.memset(ones[:, :], 1.0).then_inc(consts, 1)
            pool.wait_ge(pool_chain, 2)
            nc.gpsimd.affine_select(out=ident[:, :], in_=ident[:, :], compare_op=ALU.not_equal, fill=1.0,
                                    base=0, pattern=[[-1, P]], channel_multiplier=1).then_inc(consts, 1)
            nc.gpsimd.affine_select(out=tri[:, :, :], in_=tri[:, :, :], compare_op=ALU.is_ge, fill=MASKED,
                                    base=0, pattern=[[0, 2], [-1, P]], channel_multiplier=1).then_inc(consts, 1)
            pool.wait_ge(bias_in, 32)
            nc.gpsimd.tensor_tensor(bias_out[:, :], bo_all[:, :], b2_all[:, :], ALU.add).then_inc(pool_chain, 1)
            pool.wait_ge(pool_chain, 3)
            for s in x_in:
                pool.wait_ge(s, 16)
            for t in range(0, NT, TILES):
                last = nc.gpsimd.tensor_tensor(x_res[:, t:t + TILES, :], x_all[:, t:t + TILES, :],
                                               bias_out[:, :].unsqueeze(1).broadcast_to([P, TILES, D]), ALU.add)
            last.then_inc(res_ready, 1)

            def body(b, rep):
                for i in range(PAIRS):
                    if not 0 <= PAIRS * rep + i - 1 < PAIRS * B:
                        continue
                    wait_slot(pool, inv_ready, b, rep, i - 1)
                    j = (i - 1) % NP_BUF
                    nc.gpsimd.tensor_tensor(prob[:, j, 0, S:W], prob[:, j, 0, S:W],
                                            inv_sum[:, j, 2:3].broadcast_to([P, P]), ALU.mult)
                    nc.gpsimd.tensor_scalar(prob[:, j, 1, S:W], prob[:, j, 1, S:W], inv_sum[:, j, 3:4], 0.0,
                                            ALU.mult, ALU.add)
                    for h in range(2):
                        last = nc.gpsimd.tensor_scalar(prob[:, j, h, 0:S], prob[:, j, h, 0:S],
                                                       inv_sum[:, j, h:h + 1], 0.0, ALU.mult, ALU.add)
                    last.then_inc(prob_ready, 1)
            batches(pool, body)

        @block.scalar
        def _(act):
            act.dma_start(vec_rows[BQ:BQ + PAIRS, :], b_q.rearrange("(p two) e -> p (two e)", two=2)).then_inc(vec_in, 16)
            act.dma_start(vec_rows[BK:BK + PAIRS, :], b_k.rearrange("(p two) e -> p (two e)", two=2)).then_inc(vec_in, 16)
            act.dma_start(vec_rows[LW:LW + 1, :], ln_w.rearrange("(a d) -> a d", a=1)).then_inc(vec_in, 16)
            act.dma_start(vec_rows[LB:LB + 1, :], ln_b.rearrange("(a d) -> a d", a=1)).then_inc(vec_in, 16)
            act.dma_start(vec_rows[B1:B1 + FC, :], b1.rearrange("(c p) -> c p", p=P)).then_inc(vec_in, 16)
            act.dma_start(wv_raw[:, :].rearrange("d (h e) -> d h e", h=H),
                          w_v.rearrange("h d e -> d h e")).then_inc(w_in["v"], 16)
            act.dma_start(bv_all[:, :], b_v.rearrange("(a h) e -> a (h e)", a=1).broadcast_to([P, H * E])).then_inc(w_in["v"], 16)
            act.dma_start(w1_raw[:, :, :], w1.rearrange("(c p) d -> p c d", p=P)).then_inc(w12_in, 16)
            act.dma_start(w2_raw[:, :], w2).then_inc(w12_in, 16)
            act.dma_start(wo[:, :, :], w_o.rearrange("(p two) e d -> (two e) p d", two=2)).then_inc(wo_in, 16)

            def square_root(n, lo, hi):
                act.wait_ge(var_ready, n)
                nc.scalar.activation(std[:, lo:hi], veps[:, lo:hi], ACT.Sqrt).then_inc(std_ready, 1)

            def high_part(name):
                act.wait_ge(w_in[name], 32 if name == "v" else 16)
                nc.scalar.activation(whi[name][:, :], raw[name][:, :], ACT.Copy).then_inc(w_hi_done, 1)

            square_root(1, 0, TILES)
            high_part("q")
            square_root(2, 0, TILES)
            act.wait_ge(vecs_T, 1)
            nc.scalar.activation(vecs[:, :], ptn_ps[:, 0:NVEC], ACT.Copy).then_inc(vecs_ready, 1)
            act.wait_ge(vecs_ready, 1)
            high_part("k")

            def copy_unit(n, u, b, rep):
                _, _, kind, index, _, bank = u
                m = m_ps[bank]
                if kind in "qk":
                    wait_unit(act, b, rep, n)
                    dst, col = (qT, BQ + index) if kind == "q" else (kT, BK + index)
                    nc.scalar.activation(dst[:, index, :], m[:, 0:S], ACT.Identity,
                                         bias=vecs[:, col:col + 1]).then_inc(act_copied, 1)
                elif kind == "f":
                    wait_unit(act, b, rep, n)
                    nc.scalar.activation(hT[:, index, :], m[:, 0:S], ACT.Relu,
                                         bias=vecs[:, B1 + index:B1 + index + 1]).then_inc(act_copied, 1)
                elif kind == "x" and index == "n":
                    wait_unit(act, b, rep, n)
                    nc.scalar.activation(xnT_hi[:, :], m[:, 0:S], ACT.Copy).then_inc(xnhi_ready, 1)
                elif kind == "x":
                    wait_unit(act, b, rep, n)
                    nc.scalar.activation(x2T[:, :], m[:, 0:S], ACT.Identity, bias=vecs[:, LB:LB + 1],
                                         scale=vecs[:, LW:LW + 1]).then_inc(x2_ready, 1)

            def body(b, rep):
                for i in range(PAIRS):
                    if has_tail(rep, i):
                        j = (i - LAG) % NPT_BUF
                        prev = PAIRS * rep + i - LAG - NPT_BUF
                        if prev >= 0:
                            wait_unit(act, b, rep, WHERE["z", prev % PAIRS, prev // PAIRS])
                        wait_slot(act, ptw_ready, b, rep, i - LAG)
                        nc.scalar.activation(pT_wide[:, j, :, :], ptw_ps[:, :, :], ACT.Copy).then_inc(ptw_copied, 1)
                    if rep == -1 and i == 6:
                        high_part("v")
                        act.wait_ge(w12_in, 32)
                        nc.scalar.activation(w_abs[:, :], w1_raw[:, :, :].rearrange("p c d -> p (c d)"), ACT.Abs,
                                             accum_out=abs_sum[:, 0:1]).then_inc(act_chain, 1)
                        act.wait_ge(act_chain, 1)
                        nc.scalar.activation(w_abs[:, :], w2_raw[:, :], ACT.Abs, accum_out=abs_sum[:, 1:2])\
                            .then_inc(abs_ready, 1)
                    for n, u in slot_units(rep, i):
                        copy_unit(n, u, b, rep)
                    if has_scores(rep):
                        wait_slot(act, max_ready, b, rep, i)
                        j = i % NP_BUF
                        for h in range(2):
                            nc.scalar.activation(prob[:, j, h, 0:S], s_ps[:, i % 2, h, 0:S], ACT.Exp,
                                                 bias=neg_max[:, j, h:h + 1], scale=SCALE,
                                                 accum_out=row_sum[:, j, h:h + 1])
                            last = nc.scalar.activation(prob[:, j, h, S:W], s_ps[:, i % 2, h, S:W], ACT.Exp,
                                                        bias=neg_max[:, j, 2 + h:3 + h], scale=SCALE,
                                                        accum_out=row_sum[:, j, 2 + h:3 + h])
                        last.then_inc(exp_done, 1)
                if rep == -1:
                    act.wait_ge(w1T_ready, 1)
                    nc.scalar.activation(w1T[:, :, :].rearrange("d c p -> d (c p)"), ptn_ps[:, :], ACT.Copy)\
                        .then_inc(ffn_w_ready, 1)
                    act.wait_ge(w2T_ready, 1)
                    nc.scalar.activation(w2T[:, :, :].rearrange("p c d -> p (c d)"),
                                         ptw_ps[:, :, :].rearrange("p a b -> p (a b)"), ACT.Copy)\
                        .then_inc(ffn_w_ready, 1)
                    square_root(3, TILES, NT)
                    square_root(4, TILES, NT)
            batches(act, body)

        @block.vector
        def _(dve):
            count = [0]

            def link(ins):
                count[0] += 1
                ins.then_inc(dve_chain, 1)
                dve.wait_ge(dve_chain, count[0])

            def variances(src, mv, lo, hi):
                for t in range(lo, hi):
                    last = nc.vector.bn_stats(stats[:, t, :], src[:, t, :])
                link(last)
                for t in range(lo, hi):
                    last = nc.vector.bn_aggr(mv[:, t, :], stats[:, t, :])
                link(last)
                nc.vector.tensor_scalar(veps[:, lo:hi], mv[:, lo:hi, 1], EPS, None, ALU.add).then_inc(var_ready, 1)

            def layernorms(group, lo, hi):
                dve.wait_ge(x_in[group], 16)
                variances(x_all, mv1, lo, hi)
                dve.wait_ge(std_ready, 2 * group + 1)
                link(nc.vector.reciprocal(r1[:, lo:hi], std[:, lo:hi]))
                for t in range(lo, hi):
                    last = nc.vector.tensor_scalar(xn_all[:, t, :], x_all[:, t, :], mv1[:, t, 0:1], r1[:, t:t + 1],
                                                   ALU.subtract, ALU.mult)
                link(last)
                variances(xn_all, mv2, lo, hi)
                dve.wait_ge(std_ready, 2 * group + 2)
                link(nc.vector.reciprocal(r2[:, lo:hi], std[:, lo:hi]))

            def normalise(b):
                for t in range(TILES):
                    n = b * TILES + t
                    if isinstance(b, int):
                        tile, one = slice(n, n + 1), slice(n, n + 1)
                    else:
                        tile, one = bass.ds(n, 1), bass.ds(n, 1)
                    nc.vector.tensor_copy(xn_cur[:, t:t + 1, :], xn_all[:, tile, :])
                    last = nc.vector.tensor_scalar(xh_cur[:, t:t + 1, :], xn_all[:, tile, :], mv2[:, one, 0],
                                                   r2[:, one], ALU.subtract, ALU.mult)
                last.then_inc(norm_ready, 1)

            def low_part(name, n):
                dve.wait_ge(w_hi_done, n)
                nc.vector.tensor_tensor(wlo[name][:, :], raw[name][:, :], whi[name][:, :].bitcast(F32),
                                        ALU.subtract).then_inc(w_lo_done, 1)

            def ternary(w, dst, n):
                link(nc.vector.tensor_scalar(w_below[:, :], w, nthr[:, n:n + 1], None, ALU.is_lt))
                return nc.vector.scalar_tensor_tensor(out=dst, in0=w, scalar=thr[:, n:n + 1], in1=w_below[:, :],
                                                      op0=ALU.is_gt, op1=ALU.subtract)

            layernorms(0, 0, TILES)
            normalise(0)
            def copy_unit(n, u, b, rep):
                _, _, kind, index, ub, bank = u
                m = m_ps[bank]
                if kind == "v":
                    half, t = index
                    wait_unit(dve, b, rep, n)
                    if rep == -1:
                        dve.wait_ge(w_in["v"], 32)
                    cols = slice(half * 512, half * 512 + 512)
                    nc.vector.tensor_tensor(v[:, t, cols], m[:, :], bv_all[:, cols], ALU.add).then_inc(dve_copied, 1)
                elif kind == "x" and index == "n":
                    wait(dve, xnhi_ready, b, rep, ub + 1, 1)
                    nc.vector.tensor_tensor(xnT_lo[:, :], m[:, 0:S], xnT_hi[:, :].bitcast(F32), ALU.subtract)\
                        .then_inc(dve_copied, 1)
                elif kind == "x":
                    wait(dve, x2_ready, b, rep, ub + 1, 1)
                    nc.vector.tensor_copy(x2T_hi[:, :], x2T[:, :]).then_inc(x2hi_ready, 1)
                    wait(dve, x2hi_ready, b, rep, ub + 1, 1)
                    nc.vector.tensor_tensor(x2T_lo[:, :], x2T[:, :], x2T_hi[:, :].bitcast(F32), ALU.subtract)\
                        .then_inc(dve_copied, 1)
                elif kind == "z":
                    wait_unit(dve, b, rep, n)
                    nc.vector.tensor_copy(zT[:, index, :], m[:, 0:S]).then_inc(dve_copied, 1)
                elif kind == "o":
                    wait_unit(dve, b, rep, n)
                    if index == 0:
                        wait(dve, out_done, b, rep, 16 * (rep - 1), 16)
                    row = (b - 1) * TILES + index
                    tile = slice(row, row + 1) if isinstance(b, int) else bass.ds(row, 1)
                    nc.vector.tensor_tensor(out_sb[:, index:index + 1, :], m[:, 0:D].unsqueeze(1), x_res[:, tile, :],
                                            ALU.add).then_inc(dve_copied, 1)

            def body(b, rep):
                for i in range(PAIRS):
                    if 0 <= PAIRS * rep + i - 1 < PAIRS * B:
                        wait_slot(dve, exp_done, b, rep, i - 1)
                        j = (i - 1) % NP_BUF
                        nc.vector.reciprocal(inv_sum[:, j, :], row_sum[:, j, :]).then_inc(inv_ready, 1)
                    if has_scores(rep):
                        wait_slot(dve, scores_ready, b, rep, i)
                        sc = s_ps[:, i % 2, :, :]
                        j = i % NP_BUF
                        diag = sc[:, :, P:W]
                        mask = tri[:, :, :].rearrange("p a k -> p (a k)").unsqueeze(1).broadcast_to([P, 2, 2 * P])
                        nc.vector.tensor_tensor(diag, diag, mask, ALU.add).then_inc(masked, 1)
                        wait_slot(dve, masked, b, rep, i)
                        nc.vector.reduce_max(row_max[:, j, 0:2], sc[:, :, 0:S], AX.X)
                        nc.vector.reduce_max(row_max[:, j, 2:4], sc[:, :, S:W], AX.X).then_inc(maxed, 1)
                        wait_slot(dve, maxed, b, rep, i)
                        nc.vector.tensor_scalar(neg_max[:, j, :], row_max[:, j, :], -SCALE, None, ALU.mult)\
                            .then_inc(max_ready, 1)
                    if has_tail(rep, i):
                        wait_slot(dve, ptn_ready, b, rep, i - LAG)
                        nc.vector.tensor_copy(pT_narrow[:, (i - LAG) % NPT_BUF, :, :],
                                              ptn_ps[:, 0:S].rearrange("p (h q) -> p h q", h=2)).then_inc(ptn_copied, 1)
                    if rep == -1 and i == 6:
                        for n, name in enumerate("qkv"):
                            low_part(name, n + 1)
                    for n, u in slot_units(rep, i):
                        copy_unit(n, u, b, rep)
                    if i == 3 and 0 <= rep < B - 1:
                        normalise(b + 1)
                if rep == -1:
                    dve.wait_ge(abs_total, 1)
                    link(nc.vector.tensor_scalar(thr[:, :], ptn_ps[:, 64:66], 0.5 / (FF * D), 0.5 * EPS, ALU.mult, ALU.add))
                    link(nc.vector.tensor_scalar(nthr[:, :], thr[:, :], -1.0, None, ALU.mult))
                    link(ternary(w1_raw[:, :, :].rearrange("p c d -> p (c d)"),
                                 w1_tern[:, :, :].rearrange("p c d -> p (c d)"), 0))
                    ternary(w2_raw[:, :], w2_tern[:, :], 1).then_inc(tern_ready, 1)
                    layernorms(1, TILES, NT)
                    dve.wait_ge(res_ready, 1)
            batches(dve, body)

        @block.tensor
        def _(pe):
            pe.wait_ge(consts, 3)
            pe.wait_ge(vec_in, 16 * 5)
            nc.tensor.transpose(ptn_ps[:, 0:NVEC], vec_rows[:, :], ident[0:NVEC, 0:NVEC]).then_inc(vecs_T, 1)

            def split_product(dst, lhs_hi, lhs_lo, rhs_hi, rhs_lo):
                nc.tensor.matmul(dst, lhs_lo, rhs_hi, start=True, stop=False)
                nc.tensor.matmul(dst, lhs_hi, rhs_lo, start=False, stop=False)
                return nc.tensor.matmul(dst, lhs_hi, rhs_hi, start=False, stop=True)

            def unit(n, u, b, rep):
                _, i, kind, index, ub, bank = u
                m = m_ps[bank]
                before = same_bank_before(n)
                if before is not None:
                    wait_copy(pe, b, rep, before)
                if kind in "qk":
                    if rep == -1:
                        pe.wait_ge(w_lo_done, 1 if kind == "q" else 2)
                    if index in (0, 1):
                        wait_copy(pe, b, rep, WHERE["x", "h", ub])
                    cols = slice(index * P, index * P + P)
                    last = split_product(m[:, 0:S], whi[kind][:, cols], wlo[kind][:, cols], x2T_hi[:, :], x2T_lo[:, :])
                elif kind == "v":
                    half, t = index
                    if rep == -1:
                        pe.wait_ge(w_lo_done, 3)
                    cols, toks = slice(half * 512, half * 512 + 512), slice(t * P, t * P + P)
                    last = split_product(m[:, :], x2T_hi[:, toks], x2T_lo[:, toks], whi["v"][:, cols], wlo["v"][:, cols])
                elif kind == "f":
                    nc.tensor.matmul(m[:, 0:S], w1T[:, index, :], xnT_lo[:, :], start=True, stop=False)
                    last = nc.tensor.matmul(m[:, 0:S], w1T[:, index, :], xnT_hi[:, :], start=False, stop=True)
                elif kind == "x":
                    if index == "n":
                        wait(pe, norm_ready, b, rep, ub + 1, 1)
                    src = xn_cur if index == "n" else xh_cur
                    for t in range(TILES):
                        last = nc.tensor.transpose(m[:, t * P:t * P + P], src[:, t, :], ident[:, :])
                elif kind == "o":
                    if rep == 1 and index == 0:
                        pe.wait_ge(wo_in, 16)
                    if index == 0:
                        wait_copy(pe, b, rep, WHERE["f", FC - 1, ub])
                        wait_copy(pe, b, rep, WHERE["z", PAIRS - 1, ub])
                    toks = slice(index * P, index * P + P)
                    for c in range(FC):
                        nc.tensor.matmul(m[:, 0:D], hT[:, c, toks], w2T[:, c, :], start=(c == 0), stop=False)
                    for p in range(PAIRS):
                        last = nc.tensor.matmul(m[:, 0:D], zT[:, p, toks], wo[:, p, :], start=False, stop=(p == PAIRS - 1))
                else:
                    if index in (0, PAIRS // 2):
                        wait_copy(pe, b, rep, WHERE["v", (index // (PAIRS // 2), 1), ub])
                    wait_slot(pe, ptw_copied, b, rep, i - LAG)
                    wait_slot(pe, ptn_copied, b, rep, i - LAG)
                    j = index % NPT_BUF
                    for h in range(2):
                        cols = slice((2 * index + h) * E, (2 * index + h) * E + E)
                        nc.tensor.matmul(m[h * E:h * E + E, 0:S], v[:, 0, cols], pT_wide[:, j, h, :],
                                         start=True, stop=False)
                    for h in range(2):
                        cols = slice((2 * index + h) * E, (2 * index + h) * E + E)
                        last = nc.tensor.matmul(m[h * E:h * E + E, P:S], v[:, 1, cols], pT_narrow[:, j, h, :],
                                                start=False, stop=True)
                last.then_inc(units_ready, 1)

            def scores(b, rep, i):
                wait_copy(pe, b, rep, WHERE["k", i, rep])
                wait_slot(pe, exp_done, b, rep, i - 2)
                for part in range(2):
                    for h in range(2):
                        rows = slice(h * E, h * E + E)
                        bank = s_ps[:, i % 2, h, :]
                        if part == 0:
                            nc.tensor.matmul(bank[:, 0:S], qT[rows, i, P:S], kT[rows, i, :], start=True, stop=True)
                        else:
                            last = nc.tensor.matmul(bank[:, S:W], qT[rows, i, 0:P], kT[rows, i, 0:P],
                                                    start=True, stop=True)
                last.then_inc(scores_ready, 1)

            def transposes(b, rep, i):
                if rep == 0 and i == LAG:
                    pe.wait_ge(ffn_w_ready, 2)
                wait_slot(pe, prob_ready, b, rep, i - LAG)
                wait_slot(pe, ptw_copied, b, rep, i - LAG - 1)
                wait_slot(pe, ptn_copied, b, rep, i - LAG - 1)
                j = (i - LAG) % NP_BUF
                for h in range(2):
                    nc.tensor.transpose(ptw_ps[:, h, 0:P], prob[:, j, h, S:W], ident[:, :])
                    last = nc.tensor.transpose(ptw_ps[:, h, P:S], prob[:, j, h, 0:P], ident[:, :])
                last.then_inc(ptw_ready, 1)
                for h in range(2):
                    last = nc.tensor.transpose(ptn_ps[:, h * P:h * P + P], prob[:, j, h, P:S], ident[:, :])
                last.then_inc(ptn_ready, 1)

            def body(b, rep):
                for i in range(PAIRS):
                    if has_scores(rep):
                        scores(b, rep, i)
                    if has_tail(rep, i):
                        transposes(b, rep, i)
                    for n, u in slot_units(rep, i):
                        unit(n, u, b, rep)
                if rep == -1:
                    pe.wait_ge(abs_ready, 1)
                    pe.wait_ge(vecs_ready, 1)
                    nc.tensor.matmul(ptn_ps[:, 64:66], ones[:, :], abs_sum[:, :], start=True, stop=True).then_inc(abs_total, 1)
                    pe.wait_ge(tern_ready, 1)
                    for c in range(FC):
                        last = nc.tensor.transpose(ptn_ps[:, c * P:c * P + P], w1_tern[:, c, :], ident[:, :])
                    last.then_inc(w1T_ready, 1)
                    for c in range(FC):
                        last = nc.tensor.transpose(ptw_ps[:, c // 2, (c % 2) * P:(c % 2) * P + P],
                                                   w2_tern[:, c * P:c * P + P], ident[:, :])
                    last.then_inc(w2T_ready, 1)
            batches(pe, body)


_INS = ["L0_attn_resid_stream", "L0_attn_attn_mask", "L0_attn_W_q", "L0_attn_W_k", "L0_attn_W_v", "L0_attn_W_o",
        "L0_attn_b_q", "L0_attn_b_k", "L0_attn_b_v", "L0_attn_b_o", "L0_attn_ln_w", "L0_attn_ln_b",
        "L0_ffn_W1", "L0_ffn_b1", "L0_ffn_W2", "L0_ffn_b2"]


def kernel(**inputs):
    import concourse.bacc as bacc
    from concourse.bass_utils import run_bass_kernel_spmd

    nc = bacc.Bacc("TRN2", target_bir_lowering=False, num_devices=1)
    arrays, args = {}, []
    for name in _INS:
        a = np.ascontiguousarray(inputs[name])
        arrays[f"in_{name}"] = a
        args.append(nc.dram_tensor(f"in_{name}", a.shape, mybir.dt.from_np(a.dtype), kind="ExternalInput").ap())
    args.append(nc.dram_tensor("out", (B, S, D), F32, kind="ExternalOutput").ap())
    attention_ffn_kernel(nc, *args)
    r = run_bass_kernel_spmd(nc, [arrays], core_ids=[0])
    return r.results[0]["out"]
```

```python
import numpy as np
import concourse.bass as bass
from concourse import mybir
from contextlib import ExitStack


F32 = mybir.dt.float32
F32R = mybir.dt.float32r
ACT = mybir.ActivationFunctionType
ALU = mybir.AluOpType
AX = mybir.AxisListType

P = 128
B, S, D = 8, 256, 128
H, E = 16, 64
FF = 512
EPS = 1e-5
PAIRS = H // 2
TILES = S // P
NT = B * TILES
FC = FF // P
SCALE = E ** -0.5
MASKED = -3.0e38
HALF = [slice(0, H * E // 2), slice(H * E // 2, H * E)]
SPLITS = [("q", 0), ("k", 0), ("v", 0), ("q", 1), ("k", 1), ("v", 1)]
QK_SPLITS = [split for split in SPLITS if split[0] != "v"]
LAG_T = 3
LAG_Z = 4
LEAD = 2
NQK = 4
NP_BUF = 4
NPT_BUF = 2
LN_SLOTS = (0, 1, 2, 3, 4)
OUT_SLOT = 7
F_SLOTS = (4, 7)

ACT_AT = {"wide": [3, 2, 1, 4, 5, 4, 3, 2],
          "exp_a": [3, 3, 3, 4, 2, 3, 4, 6],
          "exp_b": [4, 3, 4, 4, 3, 3, 4, 6]}
DVE_AT = {"high": [0, 2, 0, 1, 0, 2, 1, 0],
          "narrow": [0, 2, 2, 0, 2, 3, 2, 1],
          "maxima": [4, 4, 4, 4, 5, 5, 4, 6],
          "inverse": [4, 4, 4, 4, 5, 5, 4, 6],
          "hidden": [4, 4, 4, 3, 5, 5, 4, 6],
          "ln": [4, 4, 3, 4, 4, 4, 4, 4]}
REGULAR = 2

PLAN = [
    [("q", 2, 0), ("k", 2, 0), "turn_wide", "turn_narrow", ("v", (0, 0), 0), ("z", 4, -1), "scores_a",
     "scores_b"],
    [("q", 3, 0), ("k", 3, 0), "turn_wide", "turn_narrow", ("z", 5, -1), "scores_a", ("v", (0, 1), 0),
     "scores_b"],
    [("q", 4, 0), "turn_wide", ("k", 4, 0), ("z", 6, -1), "turn_narrow", "scores_a", ("o_f", 0, -1),
     "scores_b"],
    ["turn_wide", ("q", 5, 0), "turn_narrow", ("k", 5, 0), "scores_a", ("z", 7, -1), ("o_a", 0, -1),
     "scores_b"],
    [("q", 6, 0), ("k", 6, 0), "turn_wide", "turn_narrow", ("z", 0, 0), "scores_a", ("v", (1, 0), 0),
     ("f", 0, 0), "scores_b"],
    [("q", 7, 0), ("k", 7, 0), "turn_wide", "turn_narrow", ("v", (1, 1), 0), ("x", "h", 1), "scores_a",
     "scores_b", ("z", 1, 0)],
    ["turn_wide", ("q", 0, 1), ("k", 0, 1), "turn_narrow", ("z", 2, 0), ("o_b", 0, -1), "scores_a", "scores_b"],
    [("q", 1, 1), ("k", 1, 1), "turn_wide", ("f", 1, 0), ("z", 3, 0), "turn_narrow", ("x", "n", 1),
     ("o_t", 0, -1), "scores_a", "scores_b"],
]
LAST_PLAN = [["turn_wide", "turn_narrow", ("z", 4, -1)],
             ["turn_wide", "turn_narrow", ("z", 5, -1), ("o_f", 0, -1)],
             ["turn_wide", "turn_narrow", ("z", 6, -1), ("o_a", 0, -1)],
             [("z", 7, -1), ("o_b", 0, -1), ("o_t", 0, -1)], [], [], [], []]
UNITS = [[u for u in steps if not isinstance(u, str)] for steps in PLAN]
LAST_UNITS = [[u for u in steps if not isinstance(u, str)] for steps in LAST_PLAN]
COPIER = {"q": "act", "k": "act", "v": "dve", "f": "act", "x": "dve", "z": "dve",
          "o_f": "act", "o_a": "dve", "o_b": "dve", "o_t": "dve"}
PER_BATCH = sum(len(u) for u in UNITS)


def all_units():
    out = []
    for b in range(-1, B + 1):
        n = 0
        for i in range(PAIRS):
            for kind, index, off in (LAST_UNITS if b == B else UNITS)[i]:
                if 0 <= b + off < B:
                    out.append((b, i, kind, index, b + off, n % 2))
                n += 1
    return out


ALL = all_units()
WHERE = {(u[2], u[3], u[4]): n for n, u in enumerate(ALL)}


def units_done(n):
    return n + 1


def copies_done(n):
    who = COPIER[ALL[n][2]]
    return who, sum(COPIER[u[2]] == who for u in ALL[:n + 1])


def same_bank_before(n):
    return next((m for m in range(n - 1, -1, -1) if ALL[m][5] == ALL[n][5]), None)


COPIES_PER_BATCH = {w: sum(COPIER[k] == w for u in UNITS for k, _, _ in u) for w in ("act", "dve")}


def attention_ffn_kernel(nc, resid, attn_mask, w_q, w_k, w_v, w_o, b_q, b_k, b_v, b_o, ln_w, ln_b,
                         w1, b1, w2, b2, out):
    ctx = ExitStack()
    with ctx:
        def sb(name, shape, dt=F32):
            return ctx.enter_context(nc.sbuf_tensor(name, shape, dt))

        def sem(name):
            return ctx.enter_context(nc.semaphore(name))

        ident = sb("ident", [P, P])
        ones = sb("ones", [P, P])
        causal = sb("causal", [P, S])
        wq_raw = sb("wq_raw", [P, H * E])
        wk_raw = sb("wk_raw", [P, H * E])
        wv_raw = sb("wv_raw", [P, H * E])
        raw = {"q": wq_raw, "k": wk_raw, "v": wv_raw}
        whi = {n: sb(f"w{n}_hi", [P, H * E], F32R) for n in "qkv"}
        wlo = {n: sb(f"w{n}_lo", [P, H * E], F32R) for n in "qkv"}
        wo = sb("wo", [P, PAIRS, D])
        wo_hi = sb("wo_hi", [P, PAIRS, D], F32R)
        wo_lo = sb("wo_lo", [P, PAIRS, D], F32R)
        w1_raw = sb("w1_raw", [P, FC, D])
        w2_raw = sb("w2_raw", [D, FF])
        w_abs = sb("w_abs", [P, FF])
        w_below = sb("w_below", [P, FF])
        w1T_raw = sb("w1T_raw", [D, FF])
        w2T_raw = sb("w2T_raw", [P, FC * D])
        w1T = sb("w1T", [D, FC, P], F32R)
        w2T = sb("w2T", [P, FC, D], F32R)
        abs_sum = sb("abs_sum", [P, 2])
        thr = sb("thr", [P, 2])
        nthr = sb("nthr", [P, 2])
        NVEC = 2 * PAIRS + 2 + FC
        vec_rows = sb("vec_rows", [NVEC, P])
        vecs = sb("vecs", [P, NVEC])
        BQ, BK, LW, LB, B1 = 0, PAIRS, 2 * PAIRS, 2 * PAIRS + 1, 2 * PAIRS + 2
        bv_all = sb("bv_all", [P, H * E])
        bo_all = sb("bo_all", [P, D])
        b2_all = sb("b2_all", [P, D])
        bias_out = sb("bias_out", [P, D])

        x_all = sb("x_all", [P, NT, D])
        x_res = sb("x_res", [P, NT, D])
        stats = sb("stats", [P, TILES, 6])
        mv = [sb(f"mv{n}", [P, TILES, 2]) for n in range(2)]
        veps = [sb(f"veps{n}", [P, TILES]) for n in range(2)]
        rstd = [sb(f"rstd{n}", [P, TILES]) for n in range(2)]
        power = sb("power", [P, TILES])
        xn_cur = sb("xn_cur", [P, TILES, D])
        xh_cur = sb("xh_cur", [P, TILES, D])
        xnT_hi = sb("xnT_hi", [D, S], F32R)
        xnT_lo = sb("xnT_lo", [D, S], F32R)
        x2T = sb("x2T", [D, S])
        x2T_hi = sb("x2T_hi", [D, S], F32R)
        x2T_lo = sb("x2T_lo", [D, S], F32R)
        Q_LO, Q_A, Q_B, K_A, K_B, K_LO = range(6)
        qk = sb("qk", [P, NQK, 6, S], F32R)
        qk_raw = sb("qk_raw", [P, NQK, 2, S])
        v = sb("v", [P, TILES, H * E])
        hT = sb("hT", [P, FC, S])
        hT_hi = sb("hT_hi", [P, FC, S], F32R)
        hT_lo = sb("hT_lo", [P, FC, S], F32R)
        zT_hi = sb("zT_hi", [P, PAIRS, S], F32R)
        zT_lo = sb("zT_lo", [P, PAIRS, S], F32R)
        o_part = sb("o_part", [D, S])
        out_sb = sb("out_sb", [P, TILES, D])

        W = S + P
        prob = sb("prob", [P, NP_BUF, 2, W])
        pT_wide = sb("pT_wide", [P, NPT_BUF, 2, S])
        pT_narrow = sb("pT_narrow", [P, NPT_BUF, 2, P])
        neg_max = sb("neg_max", [P, NP_BUF, 4])
        slot_mark = sb("slot_mark", [P, NP_BUF])
        row_sum = sb("row_sum", [P, NP_BUF, 4])
        inv_sum = sb("inv_sum", [P, NP_BUF, 4])

        s_ps = ctx.enter_context(nc.psum_tensor("s_ps", [P, 2, 2, 512], F32))
        ptw_ps = ctx.enter_context(nc.psum_tensor("ptw_ps", [P, 2, S], F32))
        ptn_ps = ctx.enter_context(nc.psum_tensor("ptn_ps", [P, 512], F32))
        m_ps = [ctx.enter_context(nc.psum_tensor(f"m_ps{n}", [P, 512], F32)) for n in range(2)]

        x_in = [sem(f"x_in{n}") for n in range(3)]
        w_in = {n: [sem(f"w{n}_in{half}") for half in range(2)] for n in "qkv"}
        wo_in = sem("wo_in")
        w12_in = sem("w12_in")
        vec_in = sem("vec_in")
        bias_in = sem("bias_in")
        out_bias_in = sem("out_bias_in")
        consts = sem("consts")
        pool_chain = sem("pool_chain")
        dve_chain = sem("dve_chain")
        act_chain = sem("act_chain")
        w_hi_done = sem("w_hi_done")
        w_lo_done = sem("w_lo_done")
        var_ready = sem("var_ready")
        rstd_ready = sem("rstd_ready")
        stats_done = sem("stats_done")
        mv_done = sem("mv_done")
        xn_done = sem("xn_done")
        vecs_T = sem("vecs_T")
        vecs_ready = sem("vecs_ready")
        abs_ready = sem("abs_ready")
        abs_total = sem("abs_total")
        tern_ready = sem("tern_ready")
        w1T_ready = sem("w1T_ready")
        w2T_ready = sem("w2T_ready")
        wT_copied = sem("wT_copied")
        thr_ready = sem("thr_ready")
        res_ready = sem("res_ready")
        norm_ready = sem("norm_ready")
        scores_ready = sem("scores_ready")
        max_ready = sem("max_ready")
        exp_done = sem("exp_done")
        inv_ready = sem("inv_ready")
        prob_ready = sem("prob_ready")
        ptw_ready = sem("ptw_ready")
        ptn_ready = sem("ptn_ready")
        ptw_copied = sem("ptw_copied")
        ptn_copied = sem("ptn_copied")
        units_ready = sem("units_ready")
        act_copied = sem("act_copied")
        dve_copied = sem("dve_copied")
        copied = {"act": act_copied, "dve": dve_copied}
        xnhi_ready = sem("xnhi_ready")
        x2_ready = sem("x2_ready")
        wv_lo_done = sem("wv_lo_done")
        x2hi_ready = sem("x2hi_ready")
        qk_hi = sem("qk_hi")
        qk_lo = sem("qk_lo")
        h_hi = sem("h_hi")
        h_lo = sem("h_lo")
        z_hi = sem("z_hi")
        wo_hi_done = sem("wo_hi_done")
        wo_lo_done = sem("wo_lo_done")
        qk_in = [sem(f"qk_in{n}") for n in range(NQK)]
        out_done = sem("out_done")

        def at(b, rep, value, per_batch):
            return value if isinstance(b, int) else b * per_batch + (value - rep * per_batch)

        def wait(eng, s, b, rep, value, per_batch):
            if value > 0:
                eng.wait_ge(s, at(b, rep, value, per_batch))

        def wait_slot(eng, s, b, rep, slot):
            wait(eng, s, b, rep, PAIRS * rep + slot + 1, PAIRS)

        def wait_unit(eng, b, rep, n):
            wait(eng, units_ready, b, rep, units_done(n), PER_BATCH)

        def wait_copy(eng, b, rep, n):
            who, value = copies_done(n)
            wait(eng, copied[who], b, rep, value, COPIES_PER_BATCH[who])

        def slot_units(rep, i):
            return [(n, u) for n, u in enumerate(ALL) if u[0] == rep and u[1] == i]

        def due(step, table, rep, i, position):
            if rep == B:
                return position == 0
            return min(table[step][i], len(UNITS[i])) == position

        def unit_at(rep, i, position):
            units = (LAST_UNITS if rep == B else UNITS)[i]
            if position >= len(units):
                return []
            kind, index, off = units[position]
            n = WHERE.get((kind, index, rep + off))
            return [] if n is None else [(n, ALL[n])]

        def batches(eng, body):
            for b in range(-1, REGULAR):
                body(b, b)
            with eng.Fori(REGULAR, B - 1) as b:
                body(b, REGULAR)
            body(B - 1, B - 1)
            body(B, B)

        def has_scores(rep):
            return 0 <= rep < B

        def has_pair(rep, i):
            return 0 <= PAIRS * rep + i < PAIRS * B

        def low_qk(engine, buf):
            return engine.tensor_tensor(qk[:, buf, Q_LO:K_LO + 1:K_LO - Q_LO, :], qk_raw[:, buf, :, :],
                                        qk[:, buf, Q_A:K_A + 1:K_A - Q_A, :].bitcast(F32), ALU.subtract)

        block = ctx.enter_context(nc.Block())

        @block.sync
        def _(sp):
            x_v = resid.rearrange("b (t p) d -> p (b t) d", p=P)

            def load_half(eng, n, w, half):
                heads = slice(half * H // 2, (half + 1) * H // 2)
                eng.dma_start(raw[n][:, HALF[half]].rearrange("d (h e) -> d h e", e=E),
                              w[heads].rearrange("h d e -> d h e")).then_inc(w_in[n][half], 16)

            sp.dma_start(x_all[:, 0:TILES, :], x_v[:, 0:TILES, :]).then_inc(x_in[0], 16)
            sp.dma_start(vec_rows[LW:LW + 1, :], ln_w.rearrange("(a d) -> a d", a=1)).then_inc(vec_in, 16)
            sp.dma_start(vec_rows[LB:LB + 1, :], ln_b.rearrange("(a d) -> a d", a=1)).then_inc(vec_in, 16)
            for n, w in (("q", w_q), ("k", w_k), ("v", w_v)):
                load_half(sp, n, w, 0)
            sp.dma_start(x_all[:, TILES:2 * TILES, :], x_v[:, TILES:2 * TILES, :]).then_inc(x_in[1], 16)
            sp.dma_start(w1_raw[:, :, :], w1.rearrange("(c p) d -> p c d", p=P)).then_inc(w12_in, 16)
            sp.dma_start(w2_raw[:, :], w2).then_inc(w12_in, 16)
            for n, w in (("q", w_q), ("k", w_k), ("v", w_v)):
                load_half(sp, n, w, 1)
            sp.dma_start(bv_all[:, :], b_v.rearrange("(a h) e -> a (h e)", a=1).broadcast_to([P, H * E])).then_inc(bias_in, 16)
            out_v = out.rearrange("b (t p) d -> b p t d", p=P)

            def body(b, rep):
                for i in range(PAIRS):
                    pair, ub = (i + LEAD) % PAIRS, rep + (i + LEAD) // PAIRS
                    if 0 <= ub < B:
                        wait(sp, qk_lo, b, rep, PAIRS * ub + pair + 1, PAIRS)
                        buf = pair % NQK
                        sp.dma_start(qk[E:P, buf, Q_A:K_A + 1:K_A - Q_A, :].bitcast(F32), qk[0:E, buf, Q_LO:K_A + 1:K_A - Q_LO, :].bitcast(F32))\
                            .then_inc(qk_in[buf], 16)
                        sp.dma_start(qk[0:E, buf, Q_B:K_B + 1:K_B - Q_B, :].bitcast(F32), qk[E:P, buf, Q_LO:K_B + 1:K_B - Q_LO, :].bitcast(F32))\
                            .then_inc(qk_in[buf], 16)
                    if rep == 0 and i == 0:
                        sp.dma_start(x_all[:, 2 * TILES:NT, :], x_v[:, 2 * TILES:NT, :]).then_inc(x_in[2], 16)
                        sp.dma_start(bo_all[:, :], b_o.rearrange("(a d) -> a d", a=1).broadcast_to([P, D])).then_inc(out_bias_in, 16)
                        sp.dma_start(b2_all[:, :], b2.rearrange("(a d) -> a d", a=1).broadcast_to([P, D])).then_inc(out_bias_in, 16)
                        sp.dma_start(wo[:, :, :], w_o.rearrange("(p two) e d -> (two e) p d", two=2)).then_inc(wo_in, 16)
                    if rep >= 1 and i == OUT_SLOT:
                        wait_copy(sp, b, rep, WHERE["o_t", 0, rep - 1])
                        sp.dma_start(out_v[b - 1], out_sb[:, :, :]).then_inc(out_done, 16)
            batches(sp, body)
            sp.wait_ge(out_done, 16 * B)

        @block.gpsimd
        def _(pool):
            nc.gpsimd.memset(ident[:, :], 0.0).then_inc(pool_chain, 1)
            nc.gpsimd.memset(causal[:, :], 0.0).then_inc(pool_chain, 1)
            nc.gpsimd.memset(ones[:, :], 1.0).then_inc(consts, 1)
            nc.gpsimd.memset(power[:, :], -0.5).then_inc(pool_chain, 1)
            pool.wait_ge(pool_chain, 3)
            nc.gpsimd.affine_select(out=ident[:, :], in_=ident[:, :], compare_op=ALU.not_equal, fill=1.0,
                                    base=0, pattern=[[-1, P]], channel_multiplier=1).then_inc(consts, 1)
            nc.gpsimd.affine_select(out=causal[:, P:S], in_=causal[:, P:S], compare_op=ALU.is_ge, fill=MASKED,
                                    base=0, pattern=[[-1, P]], channel_multiplier=1).then_inc(consts, 1)
            def inverse_root(n, b, rep, lb):
                wait(pool, var_ready, b, rep, 2 * lb + n + 1, 2)
                nc.gpsimd.tensor_tensor(rstd[n][:, :], veps[n][:, :], power[:, :], ALU.pow).then_inc(rstd_ready, 1)

            def body(b, rep):
                if rep == -1:
                    inverse_root(0, b, rep, 0)
                    inverse_root(1, b, rep, 0)
                if rep == -1:
                    for half in range(2):
                        pool.wait_ge(w_hi_done, SPLITS.index(("v", half)) + 1)
                        nc.gpsimd.tensor_tensor(wlo["v"][:, HALF[half]], raw["v"][:, HALF[half]],
                                                whi["v"][:, HALF[half]].bitcast(F32), ALU.subtract)\
                            .then_inc(wv_lo_done, 1)
                for i in range(PAIRS):
                    pair, ub = (i + LEAD) % PAIRS, rep + (i + LEAD) // PAIRS
                    if 0 <= ub < B and rep >= 0:
                        wait(pool, qk_hi, b, rep, PAIRS * ub + pair + 1, PAIRS)
                        buf = pair % NQK
                        low_qk(nc.gpsimd, buf).then_inc(qk_lo, 1)
                    if has_pair(rep, i - 1):
                        wait_slot(pool, inv_ready, b, rep, i - 1)
                        j = (i - 1) % NP_BUF
                        nc.gpsimd.tensor_tensor(prob[:, j, 0, S:W], prob[:, j, 0, S:W],
                                                inv_sum[:, j, 2:3].broadcast_to([P, P]), ALU.mult)
                        nc.gpsimd.tensor_scalar(prob[:, j, 1, S:W], prob[:, j, 1, S:W], inv_sum[:, j, 3:4], 0.0,
                                                ALU.mult, ALU.add)
                        for h in range(2):
                            last = nc.gpsimd.tensor_scalar(prob[:, j, h, 0:S], prob[:, j, h, 0:S],
                                                           inv_sum[:, j, h:h + 1], 0.0, ALU.mult, ALU.add)
                        last.then_inc(prob_ready, 1)
                    if has_scores(rep) and i in F_SLOTS:
                        n = F_SLOTS.index(i)
                        wait(pool, h_hi, b, rep, 2 * rep + n + 1, 2)
                        cs = slice(2 * n, 2 * n + 2)
                        nc.gpsimd.tensor_tensor(hT_lo[:, cs, :], hT[:, cs, :], hT_hi[:, cs, :].bitcast(F32),
                                                ALU.subtract).then_inc(h_lo, 1)
                    if rep == 0 and i == 5:
                        pool.wait_ge(wo_hi_done, 1)
                        nc.gpsimd.tensor_tensor(wo_lo[:, :, :], wo[:, :, :], wo_hi[:, :, :].bitcast(F32),
                                                ALU.subtract).then_inc(wo_lo_done, 1)
                    if 0 <= rep < B - 1 and i in (LN_SLOTS[1], LN_SLOTS[3]):
                        inverse_root(LN_SLOTS.index(i) // 2, b, rep, rep + 1)
                    if rep == 0 and i == 1:
                        pool.wait_ge(x_in[2], 16)
                        pool.wait_ge(out_bias_in, 32)
                        nc.gpsimd.tensor_tensor(bias_out[:, :], bo_all[:, :], b2_all[:, :], ALU.add)\
                            .then_inc(pool_chain, 1)
                        pool.wait_ge(pool_chain, 4)
                    if rep == 0 and i >= 1:
                        for t in range(i - 1, B, PAIRS - 1):
                            tiles = slice(t * TILES, t * TILES + TILES)
                            nc.gpsimd.tensor_tensor(x_res[:, tiles, :], x_all[:, tiles, :],
                                                    bias_out[:, :].unsqueeze(1).broadcast_to([P, TILES, D]),
                                                    ALU.add).then_inc(res_ready, 1)
            batches(pool, body)

        @block.scalar
        def _(act):
            act.dma_start(vec_rows[BQ:BQ + PAIRS, :], b_q.rearrange("(p two) e -> p (two e)", two=2)).then_inc(vec_in, 16)
            act.dma_start(vec_rows[BK:BK + PAIRS, :], b_k.rearrange("(p two) e -> p (two e)", two=2)).then_inc(vec_in, 16)
            act.dma_start(vec_rows[B1:B1 + FC, :], b1.rearrange("(c p) -> c p", p=P)).then_inc(vec_in, 16)

            def high_part(n):
                name, half = SPLITS[n]
                act.wait_ge(w_in[name][half], 16)
                nc.scalar.activation(whi[name][:, HALF[half]], raw[name][:, HALF[half]], ACT.Copy).then_inc(w_hi_done, 1)

            act.wait_ge(vecs_T, 1)
            nc.scalar.activation(vecs[:, :], ptn_ps[:, 0:NVEC], ACT.Copy).then_inc(vecs_ready, 1)
            act.wait_ge(vecs_ready, 1)
            high_part(0)
            high_part(1)

            def copy_unit(n, u, b, rep):
                _, _, kind, index, _, bank = u
                m = m_ps[bank]
                if kind in "qk":
                    wait_unit(act, b, rep, n)
                    to, col = (0, BQ + index) if kind == "q" else (1, BK + index)
                    nc.scalar.activation(qk_raw[:, index % NQK, to, :], m[:, 0:S], ACT.Identity,
                                         bias=vecs[:, col:col + 1]).then_inc(act_copied, 1)
                elif kind == "f":
                    wait_unit(act, b, rep, n)
                    for half in range(2):
                        c = 2 * index + half
                        last = nc.scalar.activation(hT[:, c, :], m[:, half * S:half * S + S], ACT.Relu,
                                                    bias=vecs[:, B1 + c:B1 + c + 1])
                    last.then_inc(act_copied, 1)
                elif kind == "z":
                    wait_unit(act, b, rep, n)
                    nc.scalar.activation(zT_hi[:, index, :], m[:, 0:S], ACT.Copy).then_inc(z_hi, 1)
                elif kind == "o_f":
                    wait_unit(act, b, rep, n)
                    nc.scalar.activation(o_part[:, :], m[:, 0:S], ACT.Copy).then_inc(act_copied, 1)
                elif kind == "x" and index == "n":
                    wait_unit(act, b, rep, n)
                    nc.scalar.activation(xnT_hi[:, :], m[:, 0:S], ACT.Copy).then_inc(xnhi_ready, 1)
                elif kind == "x":
                    wait_unit(act, b, rep, n)
                    nc.scalar.activation(x2T[:, :], m[:, 0:S], ACT.Identity, bias=vecs[:, LB:LB + 1],
                                         scale=vecs[:, LW:LW + 1]).then_inc(x2_ready, 1)

            def exponentials(b, rep, i, h):
                j = i % NP_BUF
                if h == 0:
                    wait_slot(act, max_ready, b, rep, i)
                nc.scalar.activation(prob[:, j, h, 0:S], s_ps[:, i % 2, h, 0:S], ACT.Exp, bias=neg_max[:, j, h:h + 1],
                                     scale=-1.0, accum_out=row_sum[:, j, h:h + 1])
                last = nc.scalar.activation(prob[:, j, h, S:W], s_ps[:, i % 2, h, S:W], ACT.Exp,
                                            bias=neg_max[:, j, 2 + h:3 + h], scale=-1.0,
                                            accum_out=row_sum[:, j, 2 + h:3 + h])
                if h == 1:
                    last.then_inc(exp_done, 1)

            def copy_wide(b, rep, i):
                prev = i - LAG_T - NPT_BUF
                if has_pair(rep, prev):
                    wait_unit(act, b, rep, WHERE["z", prev % PAIRS, rep + prev // PAIRS])
                wait_slot(act, ptw_ready, b, rep, i - LAG_T)
                nc.scalar.activation(pT_wide[:, (i - LAG_T) % NPT_BUF, :, :], ptw_ps[:, :, :], ACT.Copy)\
                    .then_inc(ptw_copied, 1)

            def prepare_ffn():
                act.wait_ge(w12_in, 32)
                nc.scalar.activation(w_abs[:, :], w1_raw[:, :, :].rearrange("p c d -> p (c d)"), ACT.Abs,
                                     accum_out=abs_sum[:, 0:1]).then_inc(act_chain, 1)
                act.wait_ge(act_chain, 1)
                nc.scalar.activation(w_abs[:, :], w2_raw[:, :], ACT.Abs, accum_out=abs_sum[:, 1:2])\
                    .then_inc(abs_ready, 1)
                act.wait_ge(w1T_ready, 1)
                nc.scalar.activation(w1T_raw[:, :], ptn_ps[:, :], ACT.Copy).then_inc(wT_copied, 1)
                act.wait_ge(w2T_ready, 1)
                nc.scalar.activation(w2T_raw[:, :], ptw_ps[:, :, :].rearrange("p a b -> p (a b)"), ACT.Copy)\
                    .then_inc(wT_copied, 1)

            def body(b, rep):
                for i in range(PAIRS):
                    if rep == -1 and i == PAIRS - LEAD:
                        high_part(2)
                    for position in range(len(UNITS[i]) + 1):
                        if has_pair(rep, i - LAG_T) and due("wide", ACT_AT, rep, i, position):
                            copy_wide(b, rep, i)
                        if has_pair(rep, i - 1) and due("exp_a", ACT_AT, rep, i, position):
                            exponentials(b, rep, i - 1, 0)
                        if has_pair(rep, i - 1) and due("exp_b", ACT_AT, rep, i, position):
                            exponentials(b, rep, i - 1, 1)
                        for n, u in unit_at(rep, i, position):
                            copy_unit(n, u, b, rep)
                    if rep == 0 and i == 0:
                        prepare_ffn()
                    if rep == 0 and i == 4:
                        act.wait_ge(wo_in, 16)
                        nc.scalar.activation(wo_hi[:, :, :], wo[:, :, :], ACT.Copy).then_inc(wo_hi_done, 1)
                if rep == -1:
                    for n in range(3, len(SPLITS)):
                        high_part(n)
            batches(act, body)

        @block.vector
        def _(dve):
            count = [0]

            def link(ins):
                count[0] += 1
                ins.then_inc(dve_chain, 1)
                dve.wait_ge(dve_chain, count[0])

            def tiles_of(b, t):
                n = b * TILES + t
                return slice(n, n + 1) if isinstance(b, int) else bass.ds(n, 1)

            def ln_statistics(n, b, rep, lb):
                for t in range(TILES):
                    src = x_all[:, tiles_of(b + (lb - rep), t), :] if n == 0 else xn_cur[:, t:t + 1, :]
                    last = nc.vector.bn_stats(stats[:, t, :], src.rearrange("p a d -> p (a d)"))
                last.then_inc(stats_done, 1)

            def ln_variance(n, b, rep, lb):
                if rep == -1:
                    dve.wait_ge(stats_done, n + 1)
                for t in range(TILES):
                    last = nc.vector.bn_aggr(mv[n][:, t, :], stats[:, t, :])
                last.then_inc(mv_done, 1)
                wait(dve, mv_done, b, rep, 2 * lb + n + 1, 2)
                nc.vector.tensor_scalar(veps[n][:, :], mv[n][:, :, 1], EPS, None, ALU.add).then_inc(var_ready, 1)

            def ln_apply(n, b, rep, lb):
                wait(dve, rstd_ready, b, rep, 2 * lb + n + 1, 2)
                dst = (xn_cur, xh_cur)[n]
                for t in range(TILES):
                    src = x_all[:, tiles_of(b + (lb - rep), t), :] if n == 0 else xn_cur[:, t:t + 1, :]
                    last = nc.vector.tensor_scalar(dst[:, t:t + 1, :], src, mv[n][:, t, 0:1], rstd[n][:, t:t + 1],
                                                   ALU.subtract, ALU.mult)
                last.then_inc(xn_done if n == 0 else norm_ready, 1)
                if n == 0:
                    wait(dve, xn_done, b, rep, lb + 1, 1)

            def ln_stage(stage, b, rep, lb):
                if stage == 0:
                    ln_statistics(0, b, rep, lb)
                elif stage == 1:
                    ln_variance(0, b, rep, lb)
                elif stage == 2:
                    ln_apply(0, b, rep, lb)
                    ln_statistics(1, b, rep, lb)
                elif stage == 3:
                    ln_variance(1, b, rep, lb)
                else:
                    ln_apply(1, b, rep, lb)

            def low_part(n):
                name, half = QK_SPLITS[n]
                dve.wait_ge(w_hi_done, SPLITS.index((name, half)) + 1)
                nc.vector.tensor_tensor(wlo[name][:, HALF[half]], raw[name][:, HALF[half]],
                                        whi[name][:, HALF[half]].bitcast(F32), ALU.subtract).then_inc(w_lo_done, 1)

            def ternary(w, dst, n):
                link(nc.vector.tensor_scalar(w_below[:, :], w, nthr[:, n:n + 1], None, ALU.is_lt))
                return nc.vector.scalar_tensor_tensor(out=dst, in0=w, scalar=thr[:, n:n + 1], in1=w_below[:, :],
                                                      op0=ALU.is_gt, op1=ALU.subtract)

            dve.wait_ge(x_in[0], 16)
            for stage in range(len(LN_SLOTS)):
                ln_stage(stage, -1, -1, 0)
                if stage >= 3:
                    low_part(stage - 3)
            def copy_unit(n, u, b, rep):
                _, _, kind, index, ub, bank = u
                m = m_ps[bank]
                if kind == "v":
                    half, t = index
                    wait_unit(dve, b, rep, n)
                    cols = slice(half * 512, half * 512 + 512)
                    nc.vector.tensor_tensor(v[:, t, cols], m[:, :], bv_all[:, cols], ALU.add).then_inc(dve_copied, 1)
                elif kind == "x" and index == "n":
                    wait(dve, xnhi_ready, b, rep, ub + 1, 1)
                    nc.vector.tensor_tensor(xnT_lo[:, :], m[:, 0:S], xnT_hi[:, :].bitcast(F32), ALU.subtract)\
                        .then_inc(dve_copied, 1)
                elif kind == "x":
                    wait(dve, x2_ready, b, rep, ub + 1, 1)
                    nc.vector.tensor_copy(x2T_hi[:, :], x2T[:, :]).then_inc(x2hi_ready, 1)
                    wait(dve, x2hi_ready, b, rep, ub + 1, 1)
                    nc.vector.tensor_tensor(x2T_lo[:, :], x2T[:, :], x2T_hi[:, :].bitcast(F32), ALU.subtract)\
                        .then_inc(dve_copied, 1)
                elif kind == "z":
                    wait_slot(dve, z_hi, b, rep, PAIRS * (ub - rep) + index)
                    nc.vector.tensor_tensor(zT_lo[:, index, :], m[:, 0:S], zT_hi[:, index, :].bitcast(F32),
                                            ALU.subtract).then_inc(dve_copied, 1)
                elif kind in ("o_a", "o_b"):
                    wait_unit(dve, b, rep, n)
                    wait_copy(dve, b, rep, WHERE["o_f" if kind == "o_a" else "o_a", 0, ub])
                    nc.vector.tensor_tensor(o_part[:, :], m[:, 0:S], o_part[:, :], ALU.add).then_inc(dve_copied, 1)
                elif kind == "o_t":
                    wait_unit(dve, b, rep, n)
                    wait(dve, out_done, b, rep, 16 * (rep - 1), 16)
                    row = (b - 1) * TILES
                    tiles = slice(row, row + TILES) if isinstance(b, int) else bass.ds(row, TILES)
                    nc.vector.tensor_tensor(out_sb[:, :, :], m[:, 0:S].rearrange("p (t d) -> p t d", d=D),
                                            x_res[:, tiles, :], ALU.add).then_inc(dve_copied, 1)

            def high_hidden(n, b, rep):
                wait_copy(dve, b, rep, WHERE["f", n, rep])
                cs = slice(2 * n, 2 * n + 2)
                nc.vector.tensor_copy(hT_hi[:, cs, :], hT[:, cs, :]).then_inc(h_hi, 1)

            def high_qk(b, rep, i):
                pair, ub = (i + LEAD) % PAIRS, rep + (i + LEAD) // PAIRS
                if not 0 <= ub < B:
                    return
                wait_copy(dve, b, rep, WHERE["k", pair, ub])
                buf = pair % NQK
                nc.vector.tensor_copy(qk[:, buf, Q_A:K_B + 1, :].rearrange("p (a h) s -> p a h s", h=2),
                                      qk_raw[:, buf, :, :].unsqueeze(2).broadcast_to([P, 2, 2, S])).then_inc(qk_hi, 1)
                if rep == -1:
                    dve.wait_ge(qk_hi, pair + 1)
                    low_qk(nc.vector, buf).then_inc(qk_lo, 1)

            def inverse_sums(b, rep, i):
                wait_slot(dve, exp_done, b, rep, i)
                j = i % NP_BUF
                nc.vector.reciprocal(inv_sum[:, j, :], row_sum[:, j, :]).then_inc(inv_ready, 1)

            def row_maxima(b, rep, i):
                wait_slot(dve, scores_ready, b, rep, i)
                j = i % NP_BUF
                nc.vector.tensor_copy(slot_mark[:, j:j + 1], causal[:, 0:1])
                for h in range(2):
                    for col, cols, mask in ((h, slice(0, S), causal[:, :]), (2 + h, slice(S, W), causal[:, P:S])):
                        sc = s_ps[:, i % 2, h, cols]
                        last = nc.vector.tensor_tensor_reduce(out=sc, in0=sc, in1=mask, scale=-SCALE, scalar=-MASKED,
                                                              op0=ALU.add, op1=ALU.min,
                                                              accum_out=neg_max[:, j, col:col + 1])
                last.then_inc(max_ready, 1)

            def copy_narrow(b, rep, i):
                wait_slot(dve, ptn_ready, b, rep, i - LAG_T)
                nc.vector.tensor_copy(pT_narrow[:, (i - LAG_T) % NPT_BUF, :, :],
                                      ptn_ps[:, 0:S].rearrange("p (h q) -> p h q", h=2)).then_inc(ptn_copied, 1)

            def thresholds():
                dve.wait_ge(abs_total, 1)
                nc.vector.tensor_scalar(thr[:, :], ptn_ps[:, 0:2], 0.5 / (FF * D), 0.5 * EPS, ALU.mult, ALU.add)\
                    .then_inc(thr_ready, 1)
                dve.wait_ge(thr_ready, 1)
                link(nc.vector.tensor_scalar(nthr[:, :], thr[:, :], -1.0, None, ALU.mult))

            def body(b, rep):
                for i in range(PAIRS):
                    if rep == 0 and i == 2:
                        thresholds()
                    if rep == 0 and i == 0:
                        low_part(2)
                        low_part(3)
                        dve.wait_ge(bias_in, 16)
                    if rep == 1 and i == 0:
                        dve.wait_ge(res_ready, B)
                    for position in range(len(UNITS[i]) + 1):
                        if due("high", DVE_AT, rep, i, position):
                            if 0 <= rep < B - 1 and i in (LN_SLOTS[1], LN_SLOTS[3]):
                                wait(dve, stats_done, b, rep, 2 * (rep + 1) + LN_SLOTS.index(i) // 2 + 1, 2)
                            high_qk(b, rep, i)
                        if has_pair(rep, i - LAG_T) and due("narrow", DVE_AT, rep, i, position):
                            copy_narrow(b, rep, i)
                        if has_scores(rep) and due("maxima", DVE_AT, rep, i, position):
                            row_maxima(b, rep, i)
                        if has_pair(rep, i - 1) and due("inverse", DVE_AT, rep, i, position):
                            inverse_sums(b, rep, i - 1)
                        if has_scores(rep) and i in F_SLOTS and due("hidden", DVE_AT, rep, i, position):
                            high_hidden(F_SLOTS.index(i), b, rep)
                        if 0 <= rep < B - 1 and i in LN_SLOTS and due("ln", DVE_AT, rep, i, position):
                            if rep in (0, 1) and i == 0:
                                dve.wait_ge(x_in[rep + 1], 16)
                            ln_stage(LN_SLOTS.index(i), b, rep, rep + 1)
                        for n, u in unit_at(rep, i, position):
                            copy_unit(n, u, b, rep)
                    if rep == 0 and i == 3:
                        dve.wait_ge(wT_copied, 2)
                        ternary(w1T_raw[:, :], w1T[:, :, :].rearrange("d c p -> d (c p)"), 0).then_inc(tern_ready, 1)
                        dve.wait_ge(tern_ready, 1)
                        ternary(w2T_raw[:, :], w2T[:, :, :].rearrange("p c d -> p (c d)"), 1).then_inc(tern_ready, 1)
            batches(dve, body)

        @block.tensor
        def _(pe):
            pe.wait_ge(consts, 3)
            pe.wait_ge(vec_in, 16 * 5)
            nc.tensor.transpose(ptn_ps[:, 0:NVEC], vec_rows[:, :], ident[0:NVEC, 0:NVEC]).then_inc(vecs_T, 1)

            def split_product(dst, lhs_hi, lhs_lo, rhs_hi, rhs_lo):
                nc.tensor.matmul(dst, lhs_lo, rhs_hi, start=True, stop=False)
                nc.tensor.matmul(dst, lhs_hi, rhs_lo, start=False, stop=False)
                return nc.tensor.matmul(dst, lhs_hi, rhs_hi, start=False, stop=True)

            def unit(n, u, b, rep):
                _, i, kind, index, ub, bank = u
                m = m_ps[bank]
                before = same_bank_before(n)
                if before is not None:
                    wait_copy(pe, b, rep, before)
                if kind in "qk":
                    if rep <= 0:
                        pe.wait_ge(w_lo_done, QK_SPLITS.index((kind, index // (PAIRS // 2))) + 1)
                    if index == 0:
                        wait_copy(pe, b, rep, WHERE["x", "h", ub])
                    cols = slice(index * P, index * P + P)
                    last = split_product(m[:, 0:S], whi[kind][:, cols], wlo[kind][:, cols], x2T_hi[:, :], x2T_lo[:, :])
                elif kind == "v":
                    half, t = index
                    if rep == 0:
                        pe.wait_ge(wv_lo_done, half + 1)
                    cols, toks = slice(half * 512, half * 512 + 512), slice(t * P, t * P + P)
                    last = split_product(m[:, :], x2T_hi[:, toks], x2T_lo[:, toks], whi["v"][:, cols], wlo["v"][:, cols])
                elif kind == "f":
                    if rep == 0:
                        pe.wait_ge(tern_ready, 1)
                    for half in range(2):
                        c, dst = 2 * index + half, m[:, half * S:half * S + S]
                        nc.tensor.matmul(dst, w1T[:, c, :], xnT_lo[:, :], start=True, stop=False)
                        last = nc.tensor.matmul(dst, w1T[:, c, :], xnT_hi[:, :], start=False, stop=True)
                elif kind == "x":
                    if index == "h":
                        wait(pe, norm_ready, b, rep, ub + 1, 1)
                    src = xn_cur if index == "n" else xh_cur
                    for t in range(TILES):
                        last = nc.tensor.transpose(m[:, t * P:t * P + P], src[:, t, :], ident[:, :])
                elif kind == "o_f":
                    if rep == 1:
                        pe.wait_ge(tern_ready, 2)
                    wait(pe, h_lo, b, rep, FC // 2 * (ub + 1), FC // 2)
                    for hidden in (hT_lo, hT_hi):
                        for c in range(FC):
                            last = nc.tensor.matmul(m[:, 0:S], w2T[:, c, :], hidden[:, c, :],
                                                    start=(hidden is hT_lo and c == 0),
                                                    stop=(hidden is hT_hi and c == FC - 1))
                elif kind in ("o_a", "o_b"):
                    if rep == 1 and kind == "o_a":
                        pe.wait_ge(wo_lo_done, 1)
                    pairs = range(PAIRS // 2) if kind == "o_a" else range(PAIRS // 2, PAIRS)
                    for p in pairs:
                        if p == pairs[0] or rep == B:
                            wait_copy(pe, b, rep, WHERE["z", p if rep == B else pairs[-1], ub])
                        nc.tensor.matmul(m[:, 0:S], wo_lo[:, p, :], zT_hi[:, p, :], start=(p == pairs[0]), stop=False)
                        nc.tensor.matmul(m[:, 0:S], wo_hi[:, p, :], zT_lo[:, p, :], start=False, stop=False)
                        last = nc.tensor.matmul(m[:, 0:S], wo_hi[:, p, :], zT_hi[:, p, :], start=False,
                                                stop=(p == pairs[-1]))
                elif kind == "o_t":
                    wait_copy(pe, b, rep, WHERE["o_b", 0, ub])
                    for t in range(TILES):
                        last = nc.tensor.transpose(m[:, t * P:t * P + P], o_part[:, t * P:t * P + P], ident[:, :])
                else:
                    if index in (0, PAIRS // 2):
                        wait_copy(pe, b, rep, WHERE["v", (index // (PAIRS // 2), 1), ub])
                    wait_slot(pe, ptw_copied, b, rep, i - LAG_Z)
                    wait_slot(pe, ptn_copied, b, rep, i - LAG_Z)
                    j = index % NPT_BUF
                    for h in range(2):
                        cols = slice((2 * index + h) * E, (2 * index + h) * E + E)
                        nc.tensor.matmul(m[h * E:h * E + E, 0:S], v[:, 0, cols], pT_wide[:, j, h, :],
                                         start=True, stop=False)
                    for h in range(2):
                        cols = slice((2 * index + h) * E, (2 * index + h) * E + E)
                        last = nc.tensor.matmul(m[h * E:h * E + E, P:S], v[:, 1, cols], pT_narrow[:, j, h, :],
                                                start=False, stop=True)
                last.then_inc(units_ready, 1)

            def scores(b, rep, i, part):
                if part == "a":
                    wait(pe, qk_in[i % NQK], b, rep, 32 * ((PAIRS * rep + i) // NQK + 1), 32 * PAIRS // NQK)
                    wait_slot(pe, exp_done, b, rep, i - 2)
                buf = i % NQK
                toks, cols = (slice(P, S), slice(0, S)) if part == "a" else (slice(0, P), slice(S, 2 * S))
                for h, (q_at, k_at) in enumerate(((Q_A, K_A), (Q_B, K_B))):
                    nc.tensor.matmul(s_ps[:, i % 2, h, cols], qk[:, buf, q_at, toks], qk[:, buf, k_at, :],
                                     start=True, stop=False)
                for h, q_at in enumerate((Q_A, Q_B)):
                    rows = slice(h * E, h * E + E)
                    last = nc.tensor.matmul(s_ps[:, i % 2, h, cols], qk[rows, buf, q_at, toks], qk[rows, buf, K_LO, :],
                                            start=False, stop=True)
                if part == "b":
                    last.then_inc(scores_ready, 1)

            def turn_wide(b, rep, i):
                if rep == 0 and i == LAG_T:
                    pe.wait_ge(wT_copied, 2)
                    pe.wait_ge(thr_ready, 1)
                wait_slot(pe, prob_ready, b, rep, i - LAG_T)
                wait_slot(pe, ptw_copied, b, rep, i - LAG_T - 1)
                j = (i - LAG_T) % NP_BUF
                for h in range(2):
                    nc.tensor.transpose(ptw_ps[:, h, 0:P], prob[:, j, h, S:W], ident[:, :])
                    last = nc.tensor.transpose(ptw_ps[:, h, P:S], prob[:, j, h, 0:P], ident[:, :])
                last.then_inc(ptw_ready, 1)

            def turn_narrow(b, rep, i):
                wait_slot(pe, ptn_copied, b, rep, i - LAG_T - 1)
                j = (i - LAG_T) % NP_BUF
                for h in range(2):
                    last = nc.tensor.transpose(ptn_ps[:, h * P:h * P + P], prob[:, j, h, P:S], ident[:, :])
                last.then_inc(ptn_ready, 1)

            def transpose_ffn():
                pe.wait_ge(w12_in, 32)
                pe.wait_ge(vecs_ready, 1)
                for c in range(FC):
                    last = nc.tensor.transpose(ptn_ps[:, c * P:c * P + P], w1_raw[:, c, :], ident[:, :])
                last.then_inc(w1T_ready, 1)
                for c in range(FC):
                    last = nc.tensor.transpose(ptw_ps[:, c // 2, (c % 2) * P:(c % 2) * P + P],
                                               w2_raw[:, c * P:c * P + P], ident[:, :])
                last.then_inc(w2T_ready, 1)

            def total_ffn():
                pe.wait_ge(abs_ready, 1)
                pe.wait_ge(wT_copied, 1)
                nc.tensor.matmul(ptn_ps[:, 0:2], ones[:, :], abs_sum[:, :], start=True, stop=True).then_inc(abs_total, 1)

            def body(b, rep):
                for i in range(PAIRS):
                    units = iter(slot_units(rep, i))
                    for step in (LAST_PLAN if rep == B else PLAN)[i]:
                        if step in ("scores_a", "scores_b"):
                            if has_scores(rep):
                                scores(b, rep, i, step[-1])
                        elif step == "turn_wide":
                            if has_pair(rep, i - LAG_T):
                                turn_wide(b, rep, i)
                        elif step == "turn_narrow":
                            if has_pair(rep, i - LAG_T):
                                turn_narrow(b, rep, i)
                        elif 0 <= rep + step[2] < B:
                            unit(*next(units), b, rep)
                    if rep == 0 and i == 0:
                        transpose_ffn()
                    if rep == 0 and i == 1:
                        total_ffn()
            batches(pe, body)


_INS = ["L0_attn_resid_stream", "L0_attn_attn_mask", "L0_attn_W_q", "L0_attn_W_k", "L0_attn_W_v", "L0_attn_W_o",
        "L0_attn_b_q", "L0_attn_b_k", "L0_attn_b_v", "L0_attn_b_o", "L0_attn_ln_w", "L0_attn_ln_b",
        "L0_ffn_W1", "L0_ffn_b1", "L0_ffn_W2", "L0_ffn_b2"]


def kernel(**inputs):
    import concourse.bacc as bacc
    from concourse.bass_utils import run_bass_kernel_spmd

    nc = bacc.Bacc("TRN2", target_bir_lowering=False, num_devices=1)
    arrays, args = {}, []
    for name in _INS:
        a = np.ascontiguousarray(inputs[name])
        arrays[f"in_{name}"] = a
        args.append(nc.dram_tensor(f"in_{name}", a.shape, mybir.dt.from_np(a.dtype), kind="ExternalInput").ap())
    args.append(nc.dram_tensor("out", (B, S, D), F32, kind="ExternalOutput").ap())
    attention_ffn_kernel(nc, *args)
    r = run_bass_kernel_spmd(nc, [arrays], core_ids=[0])
    return r.results[0]["out"]
```

```python
import numpy as np
import concourse.bass as bass
from concourse import mybir
from contextlib import ExitStack


F32 = mybir.dt.float32
F32R = mybir.dt.float32r
ACT = mybir.ActivationFunctionType
ALU = mybir.AluOpType

P = 128
B, S, D = 8, 256, 128
H, E = 16, 64
FF = 512
EPS = 1e-5
PAIRS = H // 2
TILES = S // P
NT = B * TILES
FC = FF // P
SCALE = E ** -0.5
MASKED = -3.0e38
HALF = [slice(0, H * E // 2), slice(H * E // 2, H * E)]
SPLITS = [("q", 0), ("k", 0), ("v", 0), ("q", 1), ("k", 1), ("v", 1)]
QK_SPLITS = [split for split in SPLITS if split[0] != "v"]
LAG_T = 3
LAG_Z = 4
LEAD = 2
NQK = 4
NP_BUF = 4
NPT_BUF = 2
LN_SLOTS = (0, 1, 2, 3, 4)
OUT_SLOT = 7

ACT_AT = {"wide": [3, 2, 3, 2, 3, 2, 2, 2],
          "exp_a": [3, 4, 2, 4, 2, 4, 2, 4],
          "exp_b": [4, 4, 4, 4, 3, 5, 4, 6]}
DVE_AT = {"high": [4, 0, 3, 2, 0, 3, 0, 3],
          "narrow": [0, 3, 0, 1, 4, 4, 4, 4],
          "maxima": [4, 4, 4, 4, 5, 5, 4, 6],
          "inverse": [4, 4, 4, 4, 5, 5, 4, 6],
          "hidden": [1, 0, 4, 0, 5, 0, 2, 6],
          "ln": [2, 4, 4, 2, 4, 4, 4, 5]}
POOL_ORDER = [["root", "low", "normalise", "hidden"],
              ["low", "normalise", "hidden", "root"],
              ["root", "low", "hidden", "normalise"],
              ["hidden", "low", "normalise", "root"],
              ["low", "normalise", "root", "hidden"],
              ["low", "root", "normalise", "hidden"],
              ["root", "low", "hidden", "normalise"],
              ["low", "normalise", "root", "hidden"]]
ONCE = {"v1_high": (-1, 7), "v1_low": (0, 0), "w1_ternary": (0, 3),
        "w2_ternary": (0, 5), "wo_high": (0, 5), "wo_low": (0, 5)}
REGULAR = 2

PLAN = [
    [("q", 2, 0), "turn_wide", ("k", 2, 0), "turn_narrow", ("v", (0, 0), 0), ("z", 4, -1), "scores_a",
     "scores_b"],
    [("q", 3, 0), "turn_wide", ("k", 3, 0), ("z", 5, -1), "turn_narrow", "scores_a", ("v", (0, 1), 0),
     "scores_b"],
    [("q", 4, 0), "turn_wide", ("k", 4, 0), ("z", 6, -1), "turn_narrow", ("o_f", 0, -1), "scores_a",
     "scores_b"],
    [("q", 5, 0), "turn_wide", ("k", 5, 0), ("z", 7, -1), "turn_narrow", ("o_a", 0, -1), "scores_a",
     "scores_b"],
    [("q", 6, 0), ("k", 6, 0), "turn_wide", ("z", 0, 0), ("v", (1, 0), 0), "turn_narrow", "scores_a",
     ("f", 0, 0), "scores_b"],
    [("q", 7, 0), "turn_wide", ("k", 7, 0), ("v", (1, 1), 0), "turn_narrow", ("x", "h", 1), "scores_a",
     ("z", 1, 0), "scores_b"],
    [("q", 0, 1), "turn_wide", ("k", 0, 1), "turn_narrow", ("z", 2, 0), ("o_b", 0, -1), "scores_a", "scores_b"],
    [("q", 1, 1), ("k", 1, 1), "turn_wide", ("f", 1, 0), ("z", 3, 0), "turn_narrow", "scores_a", ("o_t", 0, -1),
     ("x", "n", 1), "scores_b"],
]
LAST_PLAN = [
    ["turn_wide", "turn_narrow", ("z", 4, -1)],
    [("z", 5, -1), "turn_wide", "turn_narrow", ("o_f", 0, -1)],
    [("z", 6, -1), "turn_wide", "turn_narrow", ("o_a", 0, -1)],
    [("z", 7, -1), ("o_b", 0, -1), ("o_t", 0, -1)],
    [],
    [],
    [],
    [],
]
UNITS = [[u for u in steps if not isinstance(u, str)] for steps in PLAN]
LAST_UNITS = [[u for u in steps if not isinstance(u, str)] for steps in LAST_PLAN]
F_SLOTS = [next(i for i in range(PAIRS) if ("f", n, 0) in PLAN[i]) for n in range(FC // 2)]
COPIER = {"q": "act", "k": "act", "v": "dve", "f": "act", "x": "dve", "z": "dve",
          "o_f": "act", "o_a": "dve", "o_b": "dve", "o_t": "dve"}
PER_BATCH = sum(len(u) for u in UNITS)


def all_units():
    out = []
    for b in range(-1, B + 1):
        n = 0
        for i in range(PAIRS):
            for kind, index, off in (LAST_UNITS if b == B else UNITS)[i]:
                if 0 <= b + off < B:
                    out.append((b, i, kind, index, b + off, n % 2))
                n += 1
    return out


ALL = all_units()
WHERE = {(u[2], u[3], u[4]): n for n, u in enumerate(ALL)}


def units_done(n):
    return n + 1


def copies_done(n):
    who = COPIER[ALL[n][2]]
    return who, sum(COPIER[u[2]] == who for u in ALL[:n + 1])


def same_bank_before(n):
    return next((m for m in range(n - 1, -1, -1) if ALL[m][5] == ALL[n][5]), None)


COPIES_PER_BATCH = {w: sum(COPIER[k] == w for u in UNITS for k, _, _ in u) for w in ("act", "dve")}


def attention_ffn_kernel(nc, resid, attn_mask, w_q, w_k, w_v, w_o, b_q, b_k, b_v, b_o, ln_w, ln_b,
                         w1, b1, w2, b2, out):
    ctx = ExitStack()
    with ctx:
        def sb(name, shape, dt=F32):
            return ctx.enter_context(nc.sbuf_tensor(name, shape, dt))

        def sem(name):
            return ctx.enter_context(nc.semaphore(name))

        ident = sb("ident", [P, P])
        ones = sb("ones", [P, P])
        causal = sb("causal", [P, S])
        wq_raw = sb("wq_raw", [P, H * E])
        wk_raw = sb("wk_raw", [P, H * E])
        wv_raw = sb("wv_raw", [P, H * E])
        raw = {"q": wq_raw, "k": wk_raw, "v": wv_raw}
        whi = {n: sb(f"w{n}_hi", [P, H * E], F32R) for n in "qkv"}
        wlo = {n: sb(f"w{n}_lo", [P, H * E], F32R) for n in "qkv"}
        wo = sb("wo", [P, PAIRS, D])
        wo_hi = sb("wo_hi", [P, PAIRS, D], F32R)
        wo_lo = sb("wo_lo", [P, PAIRS, D], F32R)
        w1_raw = sb("w1_raw", [P, FC, D])
        w2_raw = sb("w2_raw", [D, FF])
        w_abs = sb("w_abs", [P, FF])
        w_below = sb("w_below", [P, FF])
        w1T_raw = sb("w1T_raw", [D, FF])
        w2T_raw = sb("w2T_raw", [P, FC * D])
        w1T = sb("w1T", [D, FC, P], F32R)
        w2T = sb("w2T", [P, FC, D], F32R)
        abs_sum = sb("abs_sum", [P, 2])
        thr = sb("thr", [P, 2])
        nthr = sb("nthr", [P, 2])
        NVEC = 2 * PAIRS + 2 + FC
        vec_rows = sb("vec_rows", [NVEC, P])
        vecs = sb("vecs", [P, NVEC])
        BQ, BK, LW, LB, B1 = 0, PAIRS, 2 * PAIRS, 2 * PAIRS + 1, 2 * PAIRS + 2
        bv_all = sb("bv_all", [P, H * E])
        out_biases = sb("out_biases", [D, 2])
        out_bias = sb("out_bias", [D, 1])

        x_all = sb("x_all", [P, NT, D])
        stats = sb("stats", [P, TILES, 6])
        mv = [sb(f"mv{n}", [P, TILES, 2]) for n in range(2)]
        veps = [sb(f"veps{n}", [P, TILES]) for n in range(2)]
        rstd = [sb(f"rstd{n}", [P, TILES]) for n in range(2)]
        power = sb("power", [P, TILES])
        xn_cur = sb("xn_cur", [P, TILES, D])
        xh_cur = sb("xh_cur", [P, TILES, D])
        xnT_hi = sb("xnT_hi", [D, S], F32R)
        xnT_lo = sb("xnT_lo", [D, S], F32R)
        x2T = sb("x2T", [D, S])
        x2T_hi = sb("x2T_hi", [D, S], F32R)
        x2T_lo = sb("x2T_lo", [D, S], F32R)
        Q_LO, Q_A, Q_B, K_A, K_B, K_LO = range(6)
        qk = sb("qk", [P, NQK, 6, S], F32R)
        qk_raw = sb("qk_raw", [P, NQK, 2, S])
        v = sb("v", [P, TILES, H * E])
        hT = sb("hT", [P, FC, S])
        hT_hi = sb("hT_hi", [P, FC, S], F32R)
        hT_lo = sb("hT_lo", [P, FC, S], F32R)
        zT_hi = sb("zT_hi", [P, PAIRS, S], F32R)
        zT_lo = sb("zT_lo", [P, PAIRS, S], F32R)
        o_part = sb("o_part", [D, S])
        out_sb = sb("out_sb", [P, TILES, D])

        W = S + P
        prob = sb("prob", [P, NP_BUF, 2, W])
        pT_wide = sb("pT_wide", [P, NPT_BUF, 2, S])
        pT_narrow = sb("pT_narrow", [P, NPT_BUF, 2, P])
        neg_max = sb("neg_max", [P, NP_BUF, 4])
        slot_mark = sb("slot_mark", [P, NP_BUF])
        row_sum = sb("row_sum", [P, NP_BUF, 4])
        inv_sum = sb("inv_sum", [P, NP_BUF, 4])

        s_ps = ctx.enter_context(nc.psum_tensor("s_ps", [P, 2, 2, 512], F32))
        ptw_ps = ctx.enter_context(nc.psum_tensor("ptw_ps", [P, 2, S], F32))
        ptn_ps = ctx.enter_context(nc.psum_tensor("ptn_ps", [P, 512], F32))
        m_ps = [ctx.enter_context(nc.psum_tensor(f"m_ps{n}", [P, 512], F32)) for n in range(2)]

        x_in = [sem(f"x_in{n}") for n in range(3)]
        w_in = {n: [sem(f"w{n}_in{half}") for half in range(2)] for n in "qkv"}
        wo_in = sem("wo_in")
        w12_in = sem("w12_in")
        vec_in = sem("vec_in")
        bias_in = sem("bias_in")
        out_bias_in = sem("out_bias_in")
        consts = sem("consts")
        pool_chain = sem("pool_chain")
        dve_chain = sem("dve_chain")
        act_chain = sem("act_chain")
        w_hi_done = sem("w_hi_done")
        w_lo_done = sem("w_lo_done")
        var_ready = sem("var_ready")
        rstd_ready = sem("rstd_ready")
        stats_done = sem("stats_done")
        mv_done = sem("mv_done")
        xn_done = sem("xn_done")
        vecs_T = sem("vecs_T")
        vecs_ready = sem("vecs_ready")
        abs_ready = sem("abs_ready")
        abs_total = sem("abs_total")
        tern_ready = sem("tern_ready")
        w1T_ready = sem("w1T_ready")
        w2T_ready = sem("w2T_ready")
        wT_copied = sem("wT_copied")
        thr_ready = sem("thr_ready")
        out_bias_ready = sem("out_bias_ready")
        norm_ready = sem("norm_ready")
        scores_ready = sem("scores_ready")
        max_ready = sem("max_ready")
        exp_done = sem("exp_done")
        inv_ready = sem("inv_ready")
        prob_ready = sem("prob_ready")
        ptw_ready = sem("ptw_ready")
        ptn_ready = sem("ptn_ready")
        ptw_copied = sem("ptw_copied")
        ptn_copied = sem("ptn_copied")
        units_ready = sem("units_ready")
        act_copied = sem("act_copied")
        dve_copied = sem("dve_copied")
        copied = {"act": act_copied, "dve": dve_copied}
        xnhi_ready = sem("xnhi_ready")
        x2_ready = sem("x2_ready")
        wv_lo_done = sem("wv_lo_done")
        x2hi_ready = sem("x2hi_ready")
        qk_hi = sem("qk_hi")
        qk_lo = sem("qk_lo")
        h_hi = sem("h_hi")
        h_lo = sem("h_lo")
        z_hi = sem("z_hi")
        wo_hi_done = sem("wo_hi_done")
        wo_lo_done = sem("wo_lo_done")
        first_in = sem("first_in")
        qk_in = [sem(f"qk_in{n}") for n in range(NQK)]
        out_done = sem("out_done")

        def at(b, rep, value, per_batch):
            return value if isinstance(b, int) else b * per_batch + (value - rep * per_batch)

        def wait(eng, s, b, rep, value, per_batch):
            if value > 0:
                eng.wait_ge(s, at(b, rep, value, per_batch))

        def wait_slot(eng, s, b, rep, slot):
            wait(eng, s, b, rep, PAIRS * rep + slot + 1, PAIRS)

        def wait_unit(eng, b, rep, n):
            wait(eng, units_ready, b, rep, units_done(n), PER_BATCH)

        def wait_copy(eng, b, rep, n):
            who, value = copies_done(n)
            wait(eng, copied[who], b, rep, value, COPIES_PER_BATCH[who])

        def slot_units(rep, i):
            return [(n, u) for n, u in enumerate(ALL) if u[0] == rep and u[1] == i]

        def due(step, table, rep, i, position):
            if rep == B:
                return position == 0
            return min(table[step][i], len(UNITS[i])) == position

        def unit_at(rep, i, position):
            units = (LAST_UNITS if rep == B else UNITS)[i]
            if position >= len(units):
                return []
            kind, index, off = units[position]
            n = WHERE.get((kind, index, rep + off))
            return [] if n is None else [(n, ALL[n])]

        def batches(eng, body):
            for b in range(-1, REGULAR):
                body(b, b)
            with eng.Fori(REGULAR, B - 1) as b:
                body(b, REGULAR)
            body(B - 1, B - 1)
            body(B, B)

        def has_scores(rep):
            return 0 <= rep < B

        def has_pair(rep, i):
            return 0 <= PAIRS * rep + i < PAIRS * B

        def low_qk(engine, buf):
            return engine.tensor_tensor(qk[:, buf, Q_LO:K_LO + 1:K_LO - Q_LO, :], qk_raw[:, buf, :, :],
                                        qk[:, buf, Q_A:K_A + 1:K_A - Q_A, :].bitcast(F32), ALU.subtract)

        def shifted(buf):
            return ((qk[E:P, buf, Q_A:K_A + 1:K_A - Q_A, :], qk[0:E, buf, Q_LO:K_A + 1:K_A - Q_LO, :]),
                    (qk[0:E, buf, Q_B:K_B + 1:K_B - Q_B, :], qk[E:P, buf, Q_LO:K_B + 1:K_B - Q_LO, :]))

        block = ctx.enter_context(nc.Block())

        @block.sync
        def _(sp):
            x_v = resid.rearrange("b (t p) d -> p (b t) d", p=P)

            def load_half(eng, n, w, half):
                heads = slice(half * H // 2, (half + 1) * H // 2)
                eng.dma_start(raw[n][:, HALF[half]].rearrange("d (h e) -> d h e", e=E),
                              w[heads].rearrange("h d e -> d h e")).then_inc(w_in[n][half], 16)

            sp.dma_start(x_all[:, 0:TILES, :], x_v[:, 0:TILES, :]).then_inc(x_in[0], 16)
            sp.dma_start(vec_rows[LW:LW + 1, :], ln_w.rearrange("(a d) -> a d", a=1)).then_inc(vec_in, 16)
            sp.dma_start(vec_rows[LB:LB + 1, :], ln_b.rearrange("(a d) -> a d", a=1)).then_inc(vec_in, 16)
            for n, w in (("q", w_q), ("k", w_k), ("v", w_v)):
                load_half(sp, n, w, 0)
            sp.dma_start(x_all[:, TILES:2 * TILES, :], x_v[:, TILES:2 * TILES, :]).then_inc(x_in[1], 16)
            sp.dma_start(w1_raw[:, :, :], w1.rearrange("(c p) d -> p c d", p=P)).then_inc(w12_in, 16)
            sp.dma_start(w2_raw[:, :], w2).then_inc(w12_in, 16)
            for n, w in (("q", w_q), ("k", w_k), ("v", w_v)):
                load_half(sp, n, w, 1)
            sp.dma_start(bv_all[:, :], b_v.rearrange("(a h) e -> a (h e)", a=1).broadcast_to([P, H * E]))\
                .then_inc(bias_in, 16)
            out_v = out.rearrange("b (t p) d -> b p t d", p=P)

            def body(b, rep):
                for i in range(PAIRS):
                    pair, ub = (i + LEAD) % PAIRS, rep + (i + LEAD) // PAIRS
                    if 0 <= ub < B and (ub, pair) != (0, 0):
                        wait(sp, qk_lo, b, rep, PAIRS * ub + pair + 1, PAIRS)
                        buf = pair % NQK
                        for to, src in shifted(buf):
                            sp.dma_start(to.bitcast(F32), src.bitcast(F32)).then_inc(qk_in[buf], 16)
                    if rep == 0 and i == 0:
                        sp.dma_start(x_all[:, 2 * TILES:NT, :], x_v[:, 2 * TILES:NT, :]).then_inc(x_in[2], 16)
                        sp.dma_start(out_biases[:, 0:1], b_o.rearrange("(d a) -> d a", a=1)).then_inc(out_bias_in, 16)
                        sp.dma_start(out_biases[:, 1:2], b2.rearrange("(d a) -> d a", a=1)).then_inc(out_bias_in, 16)
                        sp.dma_start(wo[:, :, :], w_o.rearrange("(p two) e d -> (two e) p d", two=2))\
                            .then_inc(wo_in, 16)
                    if rep >= 1 and i == OUT_SLOT:
                        wait_copy(sp, b, rep, WHERE["o_t", 0, rep - 1])
                        sp.dma_start(out_v[b - 1], out_sb[:, :, :]).then_inc(out_done, 16)
            batches(sp, body)
            sp.wait_ge(out_done, 16 * B)

        @block.gpsimd
        def _(pool):
            nc.gpsimd.memset(ident[:, :], 0.0).then_inc(pool_chain, 1)
            nc.gpsimd.memset(causal[:, :], 0.0).then_inc(pool_chain, 1)
            nc.gpsimd.memset(ones[:, :], 1.0).then_inc(consts, 1)
            nc.gpsimd.memset(power[:, :], -0.5).then_inc(pool_chain, 1)
            pool.wait_ge(pool_chain, 3)
            nc.gpsimd.affine_select(out=ident[:, :], in_=ident[:, :], compare_op=ALU.not_equal, fill=1.0,
                                    base=0, pattern=[[-1, P]], channel_multiplier=1).then_inc(consts, 1)
            nc.gpsimd.affine_select(out=causal[:, P:S], in_=causal[:, P:S], compare_op=ALU.is_ge, fill=MASKED,
                                    base=0, pattern=[[-1, P]], channel_multiplier=1).then_inc(consts, 1)
            def inverse_root(n, b, rep, lb):
                wait(pool, var_ready, b, rep, 2 * lb + n + 1, 2)
                nc.gpsimd.tensor_tensor(rstd[n][:, :], veps[n][:, :], power[:, :], ALU.pow).then_inc(rstd_ready, 1)

            def low_values(half):
                pool.wait_ge(w_hi_done, SPLITS.index(("v", half)) + 1)
                nc.gpsimd.tensor_tensor(wlo["v"][:, HALF[half]], raw["v"][:, HALF[half]],
                                        whi["v"][:, HALF[half]].bitcast(F32), ALU.subtract).then_inc(wv_lo_done, 1)

            def low_parts(b, rep, i):
                pair, ub = (i + LEAD) % PAIRS, rep + (i + LEAD) // PAIRS
                if 0 <= ub < B and (ub, pair) != (0, 0):
                    wait(pool, qk_hi, b, rep, PAIRS * ub + pair + 1, PAIRS)
                    low_qk(nc.gpsimd, pair % NQK).then_inc(qk_lo, 1)

            def normalise(b, rep, i):
                if has_pair(rep, i - 1):
                    wait_slot(pool, inv_ready, b, rep, i - 1)
                    j = (i - 1) % NP_BUF
                    nc.gpsimd.tensor_tensor(prob[:, j, 0, S:W], prob[:, j, 0, S:W],
                                            inv_sum[:, j, 2:3].broadcast_to([P, P]), ALU.mult)
                    nc.gpsimd.tensor_scalar(prob[:, j, 1, S:W], prob[:, j, 1, S:W], inv_sum[:, j, 3:4], 0.0,
                                            ALU.mult, ALU.add)
                    for h in range(2):
                        last = nc.gpsimd.tensor_scalar(prob[:, j, h, 0:S], prob[:, j, h, 0:S],
                                                       inv_sum[:, j, h:h + 1], 0.0, ALU.mult, ALU.add)
                    last.then_inc(prob_ready, 1)

            def low_hidden(b, rep, i):
                if has_scores(rep) and i in F_SLOTS:
                    n = F_SLOTS.index(i)
                    wait(pool, h_hi, b, rep, 2 * rep + n + 1, 2)
                    cs = slice(2 * n, 2 * n + 2)
                    nc.gpsimd.tensor_tensor(hT_lo[:, cs, :], hT[:, cs, :], hT_hi[:, cs, :].bitcast(F32),
                                            ALU.subtract).then_inc(h_lo, 1)

            def next_root(b, rep, i):
                if 0 <= rep < B - 1 and i in (LN_SLOTS[1], LN_SLOTS[3]):
                    inverse_root(LN_SLOTS.index(i) // 2, b, rep, rep + 1)

            def body(b, rep):
                if rep == -1:
                    inverse_root(0, b, rep, 0)
                    inverse_root(1, b, rep, 0)
                    low_values(0)
                for i in range(PAIRS):
                    for step in POOL_ORDER[i]:
                        if step == "low":
                            low_parts(b, rep, i)
                        elif step == "normalise":
                            normalise(b, rep, i)
                        elif step == "hidden":
                            low_hidden(b, rep, i)
                        else:
                            next_root(b, rep, i)
                    if (rep, i) == ONCE["v1_low"]:
                        low_values(1)
                    if (rep, i) == ONCE["wo_low"]:
                        pool.wait_ge(wo_hi_done, 1)
                        nc.gpsimd.tensor_tensor(wo_lo[:, :, :], wo[:, :, :], wo_hi[:, :, :].bitcast(F32),
                                                ALU.subtract).then_inc(wo_lo_done, 1)
                    if rep == 0 and i == 6:
                        pool.wait_ge(out_bias_in, 32)
                        nc.gpsimd.tensor_tensor(out_bias[:, :], out_biases[:, 0:1], out_biases[:, 1:2], ALU.add)\
                            .then_inc(out_bias_ready, 1)
            batches(pool, body)

        @block.scalar
        def _(act):
            act.dma_start(vec_rows[BQ:BQ + PAIRS, :], b_q.rearrange("(p two) e -> p (two e)", two=2)).then_inc(vec_in, 16)
            act.dma_start(vec_rows[BK:BK + PAIRS, :], b_k.rearrange("(p two) e -> p (two e)", two=2)).then_inc(vec_in, 16)
            act.dma_start(vec_rows[B1:B1 + FC, :], b1.rearrange("(c p) -> c p", p=P)).then_inc(vec_in, 16)

            def high_part(n):
                name, half = SPLITS[n]
                act.wait_ge(w_in[name][half], 16)
                nc.scalar.activation(whi[name][:, HALF[half]], raw[name][:, HALF[half]], ACT.Copy).then_inc(w_hi_done, 1)

            act.wait_ge(vecs_T, 1)
            nc.scalar.activation(vecs[:, :], ptn_ps[:, 0:NVEC], ACT.Copy).then_inc(vecs_ready, 1)
            act.wait_ge(vecs_ready, 1)
            high_part(0)

            def copy_unit(n, u, b, rep):
                _, _, kind, index, _, bank = u
                m = m_ps[bank]
                if kind in "qk":
                    wait_unit(act, b, rep, n)
                    to, col = (0, BQ + index) if kind == "q" else (1, BK + index)
                    nc.scalar.activation(qk_raw[:, index % NQK, to, :], m[:, 0:S], ACT.Identity,
                                         bias=vecs[:, col:col + 1]).then_inc(act_copied, 1)
                elif kind == "f":
                    wait_unit(act, b, rep, n)
                    for half in range(2):
                        c = 2 * index + half
                        last = nc.scalar.activation(hT[:, c, :], m[:, half * S:half * S + S], ACT.Relu,
                                                    bias=vecs[:, B1 + c:B1 + c + 1])
                    last.then_inc(act_copied, 1)
                elif kind == "z":
                    wait_unit(act, b, rep, n)
                    nc.scalar.activation(zT_hi[:, index, :], m[:, 0:S], ACT.Copy).then_inc(z_hi, 1)
                elif kind == "o_f":
                    wait_unit(act, b, rep, n)
                    if rep == 1:
                        act.wait_ge(out_bias_ready, 1)
                    nc.scalar.activation(o_part[:, :], m[:, 0:S], ACT.Identity, bias=out_bias[:, :])\
                        .then_inc(act_copied, 1)
                elif kind == "x" and index == "n":
                    wait_unit(act, b, rep, n)
                    nc.scalar.activation(xnT_hi[:, :], m[:, 0:S], ACT.Copy).then_inc(xnhi_ready, 1)
                elif kind == "x":
                    wait_unit(act, b, rep, n)
                    nc.scalar.activation(x2T[:, :], m[:, 0:S], ACT.Identity, bias=vecs[:, LB:LB + 1],
                                         scale=vecs[:, LW:LW + 1]).then_inc(x2_ready, 1)

            def exponentials(b, rep, i, h):
                j = i % NP_BUF
                if h == 0:
                    wait_slot(act, max_ready, b, rep, i)
                nc.scalar.activation(prob[:, j, h, 0:S], s_ps[:, i % 2, h, 0:S], ACT.Exp, bias=neg_max[:, j, h:h + 1],
                                     scale=-1.0, accum_out=row_sum[:, j, h:h + 1])
                last = nc.scalar.activation(prob[:, j, h, S:W], s_ps[:, i % 2, h, S:W], ACT.Exp,
                                            bias=neg_max[:, j, 2 + h:3 + h], scale=-1.0,
                                            accum_out=row_sum[:, j, 2 + h:3 + h])
                if h == 1:
                    last.then_inc(exp_done, 1)

            def copy_wide(b, rep, i):
                prev = i - LAG_T - NPT_BUF
                if has_pair(rep, prev):
                    wait_unit(act, b, rep, WHERE["z", prev % PAIRS, rep + prev // PAIRS])
                wait_slot(act, ptw_ready, b, rep, i - LAG_T)
                nc.scalar.activation(pT_wide[:, (i - LAG_T) % NPT_BUF, :, :], ptw_ps[:, :, :], ACT.Copy)\
                    .then_inc(ptw_copied, 1)

            def prepare_ffn():
                act.wait_ge(w12_in, 32)
                nc.scalar.activation(w_abs[:, :], w1_raw[:, :, :].rearrange("p c d -> p (c d)"), ACT.Abs,
                                     accum_out=abs_sum[:, 0:1]).then_inc(act_chain, 1)
                act.wait_ge(act_chain, 1)
                nc.scalar.activation(w_abs[:, :], w2_raw[:, :], ACT.Abs, accum_out=abs_sum[:, 1:2])\
                    .then_inc(abs_ready, 1)
                act.wait_ge(w1T_ready, 1)
                nc.scalar.activation(w1T_raw[:, :], ptn_ps[:, :], ACT.Copy).then_inc(wT_copied, 1)
                act.wait_ge(w2T_ready, 1)
                nc.scalar.activation(w2T_raw[:, :], ptw_ps[:, :, :].rearrange("p a b -> p (a b)"), ACT.Copy)\
                    .then_inc(wT_copied, 1)

            def body(b, rep):
                for i in range(PAIRS):
                    if rep == -1 and i == PAIRS - LEAD:
                        high_part(1)
                        high_part(2)
                    for position in range(len(UNITS[i]) + 1):
                        if has_pair(rep, i - LAG_T) and due("wide", ACT_AT, rep, i, position):
                            copy_wide(b, rep, i)
                        if has_pair(rep, i - 1) and due("exp_a", ACT_AT, rep, i, position):
                            exponentials(b, rep, i - 1, 0)
                        if has_pair(rep, i - 1) and due("exp_b", ACT_AT, rep, i, position):
                            exponentials(b, rep, i - 1, 1)
                        for n, u in unit_at(rep, i, position):
                            copy_unit(n, u, b, rep)
                    if rep == 0 and i == 0:
                        prepare_ffn()
                    if (rep, i) == (-1, PAIRS - 1):
                        high_part(3)
                        high_part(4)
                    if (rep, i) == ONCE["v1_high"]:
                        high_part(5)
                    if (rep, i) == ONCE["wo_high"]:
                        act.wait_ge(wo_in, 16)
                        nc.scalar.activation(wo_hi[:, :, :], wo[:, :, :], ACT.Copy).then_inc(wo_hi_done, 1)
            batches(act, body)

        @block.vector
        def _(dve):
            count = [0]

            def link(ins):
                count[0] += 1
                ins.then_inc(dve_chain, 1)
                dve.wait_ge(dve_chain, count[0])

            def tiles_of(b, t):
                n = b * TILES + t
                return slice(n, n + 1) if isinstance(b, int) else bass.ds(n, 1)

            def ln_statistics(n, b, rep, lb):
                for t in range(TILES):
                    src = x_all[:, tiles_of(b + (lb - rep), t), :] if n == 0 else xn_cur[:, t:t + 1, :]
                    last = nc.vector.bn_stats(stats[:, t, :], src.rearrange("p a d -> p (a d)"))
                last.then_inc(stats_done, 1)

            def ln_variance(n, b, rep, lb):
                if rep == -1:
                    dve.wait_ge(stats_done, n + 1)
                for t in range(TILES):
                    last = nc.vector.bn_aggr(mv[n][:, t, :], stats[:, t, :])
                last.then_inc(mv_done, 1)
                wait(dve, mv_done, b, rep, 2 * lb + n + 1, 2)
                nc.vector.tensor_scalar(veps[n][:, :], mv[n][:, :, 1], EPS, None, ALU.add).then_inc(var_ready, 1)

            def ln_apply(n, b, rep, lb):
                wait(dve, rstd_ready, b, rep, 2 * lb + n + 1, 2)
                dst = (xn_cur, xh_cur)[n]
                for t in range(TILES):
                    src = x_all[:, tiles_of(b + (lb - rep), t), :] if n == 0 else xn_cur[:, t:t + 1, :]
                    last = nc.vector.tensor_scalar(dst[:, t:t + 1, :], src, mv[n][:, t, 0:1], rstd[n][:, t:t + 1],
                                                   ALU.subtract, ALU.mult)
                last.then_inc(xn_done if n == 0 else norm_ready, 1)
                if n == 0:
                    wait(dve, xn_done, b, rep, lb + 1, 1)

            def ln_stage(stage, b, rep, lb):
                if stage == 0:
                    ln_statistics(0, b, rep, lb)
                elif stage == 1:
                    ln_variance(0, b, rep, lb)
                elif stage == 2:
                    ln_apply(0, b, rep, lb)
                    ln_statistics(1, b, rep, lb)
                elif stage == 3:
                    ln_variance(1, b, rep, lb)
                else:
                    ln_apply(1, b, rep, lb)

            def low_part(n):
                name, half = QK_SPLITS[n]
                dve.wait_ge(w_hi_done, SPLITS.index((name, half)) + 1)
                nc.vector.tensor_tensor(wlo[name][:, HALF[half]], raw[name][:, HALF[half]],
                                        whi[name][:, HALF[half]].bitcast(F32), ALU.subtract).then_inc(w_lo_done, 1)

            def ternary(w, dst, n):
                link(nc.vector.tensor_scalar(w_below[:, :], w, nthr[:, n:n + 1], None, ALU.is_lt))
                return nc.vector.scalar_tensor_tensor(out=dst, in0=w, scalar=thr[:, n:n + 1], in1=w_below[:, :],
                                                      op0=ALU.is_gt, op1=ALU.subtract)

            dve.wait_ge(x_in[0], 16)
            for stage in range(len(LN_SLOTS)):
                ln_stage(stage, -1, -1, 0)
            low_part(0)
            def copy_unit(n, u, b, rep):
                _, _, kind, index, ub, bank = u
                m = m_ps[bank]
                if kind == "v":
                    half, t = index
                    wait_unit(dve, b, rep, n)
                    cols = slice(half * 512, half * 512 + 512)
                    nc.vector.tensor_tensor(v[:, t, cols], m[:, :], bv_all[:, cols], ALU.add).then_inc(dve_copied, 1)
                elif kind == "x" and index == "n":
                    wait(dve, xnhi_ready, b, rep, ub + 1, 1)
                    nc.vector.tensor_tensor(xnT_lo[:, :], m[:, 0:S], xnT_hi[:, :].bitcast(F32), ALU.subtract)\
                        .then_inc(dve_copied, 1)
                elif kind == "x":
                    wait(dve, x2_ready, b, rep, ub + 1, 1)
                    nc.vector.tensor_copy(x2T_hi[:, :], x2T[:, :]).then_inc(x2hi_ready, 1)
                    wait(dve, x2hi_ready, b, rep, ub + 1, 1)
                    nc.vector.tensor_tensor(x2T_lo[:, :], x2T[:, :], x2T_hi[:, :].bitcast(F32), ALU.subtract)\
                        .then_inc(dve_copied, 1)
                elif kind == "z":
                    wait_slot(dve, z_hi, b, rep, PAIRS * (ub - rep) + index)
                    nc.vector.tensor_tensor(zT_lo[:, index, :], m[:, 0:S], zT_hi[:, index, :].bitcast(F32),
                                            ALU.subtract).then_inc(dve_copied, 1)
                elif kind in ("o_a", "o_b"):
                    wait_unit(dve, b, rep, n)
                    wait_copy(dve, b, rep, WHERE["o_f" if kind == "o_a" else "o_a", 0, ub])
                    nc.vector.tensor_tensor(o_part[:, :], m[:, 0:S], o_part[:, :], ALU.add).then_inc(dve_copied, 1)
                elif kind == "o_t":
                    wait_unit(dve, b, rep, n)
                    wait(dve, out_done, b, rep, 16 * (rep - 1), 16)
                    row = (b - 1) * TILES
                    tiles = slice(row, row + TILES) if isinstance(b, int) else bass.ds(row, TILES)
                    nc.vector.tensor_tensor(out_sb[:, :, :], m[:, 0:S].rearrange("p (t d) -> p t d", d=D),
                                            x_all[:, tiles, :], ALU.add).then_inc(dve_copied, 1)

            def high_hidden(n, b, rep):
                wait_copy(dve, b, rep, WHERE["f", n, rep])
                cs = slice(2 * n, 2 * n + 2)
                nc.vector.tensor_copy(hT_hi[:, cs, :], hT[:, cs, :]).then_inc(h_hi, 1)

            def high_qk(b, rep, i):
                pair, ub = (i + LEAD) % PAIRS, rep + (i + LEAD) // PAIRS
                if not 0 <= ub < B:
                    return
                wait_copy(dve, b, rep, WHERE["k", pair, ub])
                buf = pair % NQK
                nc.vector.tensor_copy(qk[:, buf, Q_A:K_B + 1, :].rearrange("p (a h) s -> p a h s", h=2),
                                      qk_raw[:, buf, :, :].unsqueeze(2).broadcast_to([P, 2, 2, S])).then_inc(qk_hi, 1)
                if (ub, pair) == (0, 0):
                    dve.wait_ge(qk_hi, 1)
                    low_qk(nc.vector, buf).then_inc(qk_lo, 1)
                    dve.wait_ge(qk_lo, 1)
                    for to, src in shifted(buf):
                        last = nc.vector.tensor_copy(to, src)
                    last.then_inc(first_in, 1)

            def inverse_sums(b, rep, i):
                wait_slot(dve, exp_done, b, rep, i)
                j = i % NP_BUF
                nc.vector.reciprocal(inv_sum[:, j, :], row_sum[:, j, :]).then_inc(inv_ready, 1)

            def row_maxima(b, rep, i):
                wait_slot(dve, scores_ready, b, rep, i)
                j = i % NP_BUF
                nc.vector.tensor_copy(slot_mark[:, j:j + 1], causal[:, 0:1])
                for h in range(2):
                    for col, cols, mask in ((h, slice(0, S), causal[:, :]), (2 + h, slice(S, W), causal[:, P:S])):
                        sc = s_ps[:, i % 2, h, cols]
                        last = nc.vector.tensor_tensor_reduce(out=sc, in0=sc, in1=mask, scale=-SCALE, scalar=-MASKED,
                                                              op0=ALU.add, op1=ALU.min,
                                                              accum_out=neg_max[:, j, col:col + 1])
                last.then_inc(max_ready, 1)

            def copy_narrow(b, rep, i):
                wait_slot(dve, ptn_ready, b, rep, i - LAG_T)
                nc.vector.tensor_copy(pT_narrow[:, (i - LAG_T) % NPT_BUF, :, :],
                                      ptn_ps[:, 0:S].rearrange("p (h q) -> p h q", h=2)).then_inc(ptn_copied, 1)

            def thresholds():
                dve.wait_ge(abs_total, 1)
                nc.vector.tensor_scalar(thr[:, :], ptn_ps[:, 0:2], 0.5 / (FF * D), 0.5 * EPS, ALU.mult, ALU.add)\
                    .then_inc(thr_ready, 1)
                dve.wait_ge(thr_ready, 1)
                link(nc.vector.tensor_scalar(nthr[:, :], thr[:, :], -1.0, None, ALU.mult))

            def body(b, rep):
                for i in range(PAIRS):
                    if rep == 0 and i == 2:
                        thresholds()
                    if rep == 0 and i == 0:
                        row_maxima(b, rep, i)
                        low_part(2)
                        low_part(3)
                        dve.wait_ge(bias_in, 16)
                    if rep == -1 and i == PAIRS - LEAD:
                        low_part(1)
                    for position in range(len(UNITS[i]) + 1):
                        if due("high", DVE_AT, rep, i, position):
                            if 0 <= rep < B - 1 and i in (LN_SLOTS[1], LN_SLOTS[3]):
                                wait(dve, stats_done, b, rep, 2 * (rep + 1) + LN_SLOTS.index(i) // 2 + 1, 2)
                            high_qk(b, rep, i)
                        if has_pair(rep, i - LAG_T) and due("narrow", DVE_AT, rep, i, position):
                            copy_narrow(b, rep, i)
                        if has_scores(rep) and (rep, i) != (0, 0) and due("maxima", DVE_AT, rep, i, position):
                            row_maxima(b, rep, i)
                        if has_pair(rep, i - 1) and due("inverse", DVE_AT, rep, i, position):
                            inverse_sums(b, rep, i - 1)
                        if has_scores(rep) and i in F_SLOTS and due("hidden", DVE_AT, rep, i, position):
                            high_hidden(F_SLOTS.index(i), b, rep)
                        if 0 <= rep < B - 1 and i in LN_SLOTS and due("ln", DVE_AT, rep, i, position):
                            if rep in (0, 1) and i == 0:
                                dve.wait_ge(x_in[rep + 1], 16)
                            ln_stage(LN_SLOTS.index(i), b, rep, rep + 1)
                        for n, u in unit_at(rep, i, position):
                            copy_unit(n, u, b, rep)
                    if (rep, i) == ONCE["w1_ternary"]:
                        dve.wait_ge(wT_copied, 2)
                        ternary(w1T_raw[:, :], w1T[:, :, :].rearrange("d c p -> d (c p)"), 0).then_inc(tern_ready, 1)
                    if (rep, i) == ONCE["w2_ternary"]:
                        dve.wait_ge(tern_ready, 1)
                        ternary(w2T_raw[:, :], w2T[:, :, :].rearrange("p c d -> p (c d)"), 1).then_inc(tern_ready, 1)
            batches(dve, body)

        @block.tensor
        def _(pe):
            pe.wait_ge(consts, 3)
            pe.wait_ge(vec_in, 16 * 5)
            nc.tensor.transpose(ptn_ps[:, 0:NVEC], vec_rows[:, :], ident[0:NVEC, 0:NVEC]).then_inc(vecs_T, 1)

            def project(b, rep, ub, dst, weight_hi, weight_lo, first):
                if first:
                    wait(pe, x2hi_ready, b, rep, ub + 1, 1)
                nc.tensor.matmul(dst, weight_lo, x2T_hi[:, :], start=True, stop=False)
                nc.tensor.matmul(dst, weight_hi, x2T_hi[:, :], start=False, stop=False)
                if first:
                    wait_copy(pe, b, rep, WHERE["x", "h", ub])
                return nc.tensor.matmul(dst, weight_hi, x2T_lo[:, :], start=False, stop=True)

            def unit(n, u, b, rep):
                _, i, kind, index, ub, bank = u
                m = m_ps[bank]
                before = same_bank_before(n)
                if before is not None and ALL[before][2:4] == ("x", "h"):
                    wait(pe, x2_ready, b, rep, ALL[before][4] + 1, 1)
                elif before is not None:
                    wait_copy(pe, b, rep, before)
                if kind in "qk":
                    if rep <= 0:
                        pe.wait_ge(w_lo_done, QK_SPLITS.index((kind, index // (PAIRS // 2))) + 1)
                    cols = slice(index * P, index * P + P)
                    last = project(b, rep, ub, m[:, 0:S], whi[kind][:, cols], wlo[kind][:, cols],
                                   first=(kind == "q" and index == 0))
                elif kind == "v":
                    half, t = index
                    if rep == 0:
                        pe.wait_ge(wv_lo_done, half + 1)
                    cols, toks = slice(half * 512, half * 512 + 512), slice(t * P, t * P + P)
                    nc.tensor.matmul(m[:, :], x2T_lo[:, toks], whi["v"][:, cols], start=True, stop=False)
                    nc.tensor.matmul(m[:, :], x2T_hi[:, toks], wlo["v"][:, cols], start=False, stop=False)
                    last = nc.tensor.matmul(m[:, :], x2T_hi[:, toks], whi["v"][:, cols], start=False, stop=True)
                elif kind == "f":
                    if rep == 0:
                        pe.wait_ge(tern_ready, 1)
                    for half in range(2):
                        c, dst = 2 * index + half, m[:, half * S:half * S + S]
                        nc.tensor.matmul(dst, w1T[:, c, :], xnT_lo[:, :], start=True, stop=False)
                        last = nc.tensor.matmul(dst, w1T[:, c, :], xnT_hi[:, :], start=False, stop=True)
                elif kind == "x":
                    if index == "h":
                        wait(pe, norm_ready, b, rep, ub + 1, 1)
                    src = xn_cur if index == "n" else xh_cur
                    for t in range(TILES):
                        last = nc.tensor.transpose(m[:, t * P:t * P + P], src[:, t, :], ident[:, :])
                elif kind == "o_f":
                    if rep == 1:
                        pe.wait_ge(tern_ready, 2)
                    for s, hidden in ((h_hi, hT_hi), (h_lo, hT_lo)):
                        wait(pe, s, b, rep, FC // 2 * (ub + 1), FC // 2)
                        for c in range(FC):
                            last = nc.tensor.matmul(m[:, 0:S], w2T[:, c, :], hidden[:, c, :],
                                                    start=(hidden is hT_hi and c == 0),
                                                    stop=(hidden is hT_lo and c == FC - 1))
                elif kind in ("o_a", "o_b"):
                    if rep == 1 and kind == "o_a":
                        pe.wait_ge(wo_lo_done, 1)
                    pairs = range(PAIRS // 2) if kind == "o_a" else range(PAIRS // 2, PAIRS)
                    for p in pairs:
                        if p == pairs[0] or rep == B:
                            wait_copy(pe, b, rep, WHERE["z", p if rep == B else pairs[-1], ub])
                        nc.tensor.matmul(m[:, 0:S], wo_lo[:, p, :], zT_hi[:, p, :], start=(p == pairs[0]), stop=False)
                        nc.tensor.matmul(m[:, 0:S], wo_hi[:, p, :], zT_lo[:, p, :], start=False, stop=False)
                        last = nc.tensor.matmul(m[:, 0:S], wo_hi[:, p, :], zT_hi[:, p, :], start=False,
                                                stop=(p == pairs[-1]))
                elif kind == "o_t":
                    wait_copy(pe, b, rep, WHERE["o_b", 0, ub])
                    for t in range(TILES):
                        last = nc.tensor.transpose(m[:, t * P:t * P + P], o_part[:, t * P:t * P + P], ident[:, :])
                else:
                    if index in (0, PAIRS // 2):
                        wait_copy(pe, b, rep, WHERE["v", (index // (PAIRS // 2), 1), ub])
                    wait_slot(pe, ptw_copied, b, rep, i - LAG_Z)
                    wait_slot(pe, ptn_copied, b, rep, i - LAG_Z)
                    j = index % NPT_BUF
                    for h in range(2):
                        cols = slice((2 * index + h) * E, (2 * index + h) * E + E)
                        nc.tensor.matmul(m[h * E:h * E + E, 0:S], v[:, 0, cols], pT_wide[:, j, h, :],
                                         start=True, stop=False)
                    for h in range(2):
                        cols = slice((2 * index + h) * E, (2 * index + h) * E + E)
                        last = nc.tensor.matmul(m[h * E:h * E + E, P:S], v[:, 1, cols], pT_narrow[:, j, h, :],
                                                start=False, stop=True)
                last.then_inc(units_ready, 1)

            def scores(b, rep, i, part):
                if part == "a":
                    if (rep, i) == (0, 0):
                        pe.wait_ge(first_in, 1)
                    wait(pe, qk_in[i % NQK], b, rep, 32 * ((PAIRS * rep + i) // NQK + (i % NQK > 0)), 32 * PAIRS // NQK)
                    wait_slot(pe, exp_done, b, rep, i - 2)
                buf = i % NQK
                toks, cols = (slice(P, S), slice(0, S)) if part == "a" else (slice(0, P), slice(S, 2 * S))
                for h, (q_at, k_at) in enumerate(((Q_A, K_A), (Q_B, K_B))):
                    nc.tensor.matmul(s_ps[:, i % 2, h, cols], qk[:, buf, q_at, toks], qk[:, buf, k_at, :],
                                     start=True, stop=False)
                for h, q_at in enumerate((Q_A, Q_B)):
                    rows = slice(h * E, h * E + E)
                    last = nc.tensor.matmul(s_ps[:, i % 2, h, cols], qk[rows, buf, q_at, toks], qk[rows, buf, K_LO, :],
                                            start=False, stop=True)
                if part == "b":
                    last.then_inc(scores_ready, 1)

            def turn_wide(b, rep, i):
                if rep == 0 and i == LAG_T:
                    pe.wait_ge(wT_copied, 2)
                    pe.wait_ge(thr_ready, 1)
                wait_slot(pe, prob_ready, b, rep, i - LAG_T)
                wait_slot(pe, ptw_copied, b, rep, i - LAG_T - 1)
                j = (i - LAG_T) % NP_BUF
                for h in range(2):
                    nc.tensor.transpose(ptw_ps[:, h, 0:P], prob[:, j, h, S:W], ident[:, :])
                    last = nc.tensor.transpose(ptw_ps[:, h, P:S], prob[:, j, h, 0:P], ident[:, :])
                last.then_inc(ptw_ready, 1)

            def turn_narrow(b, rep, i):
                wait_slot(pe, ptn_copied, b, rep, i - LAG_T - 1)
                j = (i - LAG_T) % NP_BUF
                for h in range(2):
                    last = nc.tensor.transpose(ptn_ps[:, h * P:h * P + P], prob[:, j, h, P:S], ident[:, :])
                last.then_inc(ptn_ready, 1)

            def transpose_ffn():
                pe.wait_ge(w12_in, 32)
                pe.wait_ge(vecs_ready, 1)
                for c in range(FC):
                    last = nc.tensor.transpose(ptn_ps[:, c * P:c * P + P], w1_raw[:, c, :], ident[:, :])
                last.then_inc(w1T_ready, 1)
                for c in range(FC):
                    last = nc.tensor.transpose(ptw_ps[:, c // 2, (c % 2) * P:(c % 2) * P + P],
                                               w2_raw[:, c * P:c * P + P], ident[:, :])
                last.then_inc(w2T_ready, 1)

            def total_ffn():
                pe.wait_ge(abs_ready, 1)
                pe.wait_ge(wT_copied, 1)
                nc.tensor.matmul(ptn_ps[:, 0:2], ones[:, :], abs_sum[:, :], start=True, stop=True).then_inc(abs_total, 1)

            def body(b, rep):
                for i in range(PAIRS):
                    units = iter(slot_units(rep, i))
                    steps = (LAST_PLAN if rep == B else PLAN)[i]
                    if (rep, i) == (0, 0):
                        steps = ["scores_a", "scores_b"] + [s for s in steps if s not in ("scores_a", "scores_b")]
                    for step in steps:
                        if step in ("scores_a", "scores_b"):
                            if has_scores(rep):
                                scores(b, rep, i, step[-1])
                        elif step == "turn_wide":
                            if has_pair(rep, i - LAG_T):
                                turn_wide(b, rep, i)
                        elif step == "turn_narrow":
                            if has_pair(rep, i - LAG_T):
                                turn_narrow(b, rep, i)
                        elif 0 <= rep + step[2] < B:
                            unit(*next(units), b, rep)
                    if rep == 0 and i == 0:
                        transpose_ffn()
                    if rep == 0 and i == 1:
                        total_ffn()
            batches(pe, body)


_INS = ["L0_attn_resid_stream", "L0_attn_attn_mask", "L0_attn_W_q", "L0_attn_W_k", "L0_attn_W_v", "L0_attn_W_o",
        "L0_attn_b_q", "L0_attn_b_k", "L0_attn_b_v", "L0_attn_b_o", "L0_attn_ln_w", "L0_attn_ln_b",
        "L0_ffn_W1", "L0_ffn_b1", "L0_ffn_W2", "L0_ffn_b2"]


def kernel(**inputs):
    import concourse.bacc as bacc
    from concourse.bass_utils import run_bass_kernel_spmd

    nc = bacc.Bacc("TRN2", target_bir_lowering=False, num_devices=1)
    arrays, args = {}, []
    for name in _INS:
        a = np.ascontiguousarray(inputs[name])
        arrays[f"in_{name}"] = a
        args.append(nc.dram_tensor(f"in_{name}", a.shape, mybir.dt.from_np(a.dtype), kind="ExternalInput").ap())
    args.append(nc.dram_tensor("out", (B, S, D), F32, kind="ExternalOutput").ap())
    attention_ffn_kernel(nc, *args)
    r = run_bass_kernel_spmd(nc, [arrays], core_ids=[0])
    return r.results[0]["out"]
```
